# Optimizing a Trainium2 kernel written in Bass

```python
import numpy as np
import jax
import jax.numpy as jnp

def _softmax(x, axis=-1):
    return jax.nn.softmax(x, axis=axis)

def _gelu(x):
    return jax.nn.gelu(x, approximate=True)

def _silu(x):
    return jax.nn.silu(x)

def _sigmoid(x):
    return jax.nn.sigmoid(x)

def _layernorm(x, axis=-1, eps=1e-05):
    m = jnp.mean(x, axis=axis, keepdims=True)
    v = jnp.var(x, axis=axis, keepdims=True)
    return (x - m) / jnp.sqrt(v + eps)

def _scatter_add(tgt, idx, src, axis=0):
    return tgt.at[idx].add(src)

def _segment_sum(src, seg, n):
    return jax.ops.segment_sum(src, seg, n)
kernel_name = 'mk_cond_seq_d1_seqx_r4_31f89e'

def setup_inputs(seed: int=0):
    np.random.seed(seed)
    _w = jnp.asarray

    def _rec_inputs():
        import jax
        import jax.numpy as jnp
        _rk = jax.random.key(seed)
        x = 7.22e-05 + 1 * jax.random.normal(jax.random.fold_in(_rk, 1), (8, 512, 256), jnp.float32)
        _lenS = 512 - jax.random.randint(jax.random.fold_in(_rk, 7), (8,), 0, max(1, 512 // 4) + 1, jnp.int32)
        _lenS2 = 512 - jax.random.randint(jax.random.fold_in(_rk, 8), (8,), 0, max(1, 512 // 4) + 1, jnp.int32)
        cond_2048 = 0.00782532 + 1.00527 * jax.random.normal(jax.random.fold_in(_rk, 11), (8, 512), jnp.float32)
        _validS = jnp.arange(512)[None, :] < _lenS[:, None]
        _validS2 = jnp.arange(512)[None, :] < _lenS2[:, None]
        _causal = jnp.tril(jnp.ones((512, 512), dtype=bool))
        mask_BxSx1_fk1 = jnp.where(jnp.ones((8, 512, 1), dtype=bool), 1.0, 0.0).astype(jnp.float32)
        return (x, cond_2048, mask_BxSx1_fk1)
    x, cond_2048, mask_BxSx1_fk1 = _rec_inputs()

    def _L0_cond_setup():
        import jax, jax.numpy as jnp
        import numpy as np
        B, T, D, H, TE = (4, 512, 256, 8, 512)
        EPS = 1e-05

        def _ln(x, w, b):
            m = jnp.mean(x, axis=-1, keepdims=True)
            v = jnp.mean((x - m) ** 2, axis=-1, keepdims=True)
            return (x - m) * jax.lax.rsqrt(v + EPS) * w + b
        key = jax.random.key(seed)
        ks = jax.random.split(key, 16)
        s = 0.02
        inp = {'x': jax.random.normal(ks[0], (B, T, D), jnp.float32), 'emb': jax.random.normal(ks[1], (B, TE), jnp.float32), 'src_mask': (jax.random.uniform(ks[2], (B, T, 1)) > 0.2).astype(jnp.float32), 'num_head': H, 'ln_w': jnp.ones((D,), jnp.float32), 'ln_b': jnp.zeros((D,), jnp.float32), 'Wq': jax.random.normal(ks[3], (D, D), jnp.float32) * s, 'bq': jnp.zeros((D,), jnp.float32), 'Wk': jax.random.normal(ks[4], (D, D), jnp.float32) * s, 'bk': jnp.zeros((D,), jnp.float32), 'Wv': jax.random.normal(ks[5], (D, D), jnp.float32) * s, 'bv': jnp.zeros((D,), jnp.float32), 'W_emb': jax.random.normal(ks[6], (TE, 2 * D), jnp.float32) * s, 'b_emb': jnp.zeros((2 * D,), jnp.float32), 'ln2_w': jnp.ones((D,), jnp.float32), 'ln2_b': jnp.zeros((D,), jnp.float32), 'W_out': jax.random.normal(ks[7], (D, D), jnp.float32) * s, 'b_out': jnp.zeros((D,), jnp.float32)}
        return inp
    _L0_cond_all = _L0_cond_setup()
    _L0_cond_in = {k: v for k, v in _L0_cond_all.items() if k in ('ln_w', 'ln_b', 'Wq', 'bq', 'Wk', 'bk', 'Wv', 'bv', 'W_emb', 'b_emb', 'ln2_w', 'ln2_b', 'W_out', 'b_out')}
    del _L0_cond_all
    return {'x': x, 'cond_2048': cond_2048, 'mask_BxSx1_fk1': mask_BxSx1_fk1, 'L0_cond_ln_w': _L0_cond_in['ln_w'], 'L0_cond_ln_b': _L0_cond_in['ln_b'], 'L0_cond_Wq': _L0_cond_in['Wq'], 'L0_cond_bq': _L0_cond_in['bq'], 'L0_cond_Wk': _L0_cond_in['Wk'], 'L0_cond_bk': _L0_cond_in['bk'], 'L0_cond_Wv': _L0_cond_in['Wv'], 'L0_cond_bv': _L0_cond_in['bv'], 'L0_cond_W_emb': _L0_cond_in['W_emb'], 'L0_cond_b_emb': _L0_cond_in['b_emb'], 'L0_cond_ln2_w': _L0_cond_in['ln2_w'], 'L0_cond_ln2_b': _L0_cond_in['ln2_b'], 'L0_cond_W_out': _L0_cond_in['W_out'], 'L0_cond_b_out': _L0_cond_in['b_out']}

def reference(x, cond_2048, mask_BxSx1_fk1, L0_cond_ln_w, L0_cond_ln_b, L0_cond_Wq, L0_cond_bq, L0_cond_Wk, L0_cond_bk, L0_cond_Wv, L0_cond_bv, L0_cond_W_emb, L0_cond_b_emb, L0_cond_ln2_w, L0_cond_ln2_b, L0_cond_W_out, L0_cond_b_out):
    import jax
    import jax.numpy as jnp

    def _L0_cond_ref(x, emb, src_mask, num_head, ln_w, ln_b, Wq, bq, Wk, bk, Wv, bv, W_emb, b_emb, ln2_w, ln2_b, W_out, b_out):
        import jax, jax.numpy as jnp
        import numpy as np
        B, T, D, H, TE = (4, 512, 256, 8, 512)
        EPS = 1e-05

        def _ln(x, w, b):
            m = jnp.mean(x, axis=-1, keepdims=True)
            v = jnp.mean((x - m) ** 2, axis=-1, keepdims=True)
            return (x - m) * jax.lax.rsqrt(v + EPS) * w + b
        b, t, d = x.shape
        h = num_head
        dh = d // h
        xn = _ln(x, ln_w, ln_b)
        q = xn @ Wq + bq
        k = xn @ Wk + bk + (1.0 - src_mask) * -1000000.0
        q = jax.nn.softmax(q.reshape(b, t, h, dh), axis=-1)
        k = jax.nn.softmax(k.reshape(b, t, h, dh), axis=1)
        v = ((xn @ Wv + bv) * src_mask).reshape(b, t, h, dh)
        att = jnp.einsum('bnhd,bnhl->bhdl', k, v)
        y = jnp.einsum('bnhd,bhdl->bnhl', q, att).reshape(b, t, d)
        emb_out = (jax.nn.silu(emb) @ W_emb + b_emb)[:, None, :]
        scale, shift = jnp.split(emb_out, 2, axis=2)
        hh = _ln(y, ln2_w, ln2_b) * (1.0 + scale) + shift
        hh = jax.nn.silu(hh) @ W_out + b_out
        return x + hh
    x = _L0_cond_ref(x, cond_2048, mask_BxSx1_fk1, 8, L0_cond_ln_w, L0_cond_ln_b, L0_cond_Wq, L0_cond_bq, L0_cond_Wk, L0_cond_bk, L0_cond_Wv, L0_cond_bv, L0_cond_W_emb, L0_cond_b_emb, L0_cond_ln2_w, L0_cond_ln2_b, L0_cond_W_out, L0_cond_b_out)
    return x

_drawn_inputs = setup_inputs


def setup_inputs(seed=0):
    import zlib

    import numpy as np

    out = dict(_drawn_inputs(seed))
    spreads = {'L0_cond_ln_w': (1.0, 0.6),
     'L0_cond_ln_b': (0.0, 0.1),
     'L0_cond_bq': (0.0, 0.8),
     'L0_cond_bk': (0.0, 0.8),
     'L0_cond_bv': (0.0, 0.1),
     'L0_cond_b_emb': (0.0, 0.1),
     'L0_cond_ln2_w': (1.0, 0.2),
     'L0_cond_ln2_b': (0.0, 0.477),
     'L0_cond_b_out': (0.0, 0.1)}
    factors = {'L0_cond_Wq': 8.0, 'L0_cond_Wk': 8.0}
    for name, (base, spread) in spreads.items():
        noise = np.random.default_rng([zlib.crc32(name.encode()), seed]).standard_normal(out[name].shape)
        drawn = base * np.exp(spread * noise) if base else spread * noise
        out[name] = jnp.asarray(drawn.astype(out[name].dtype))
    for name, factor in factors.items():
        out[name] = (out[name] * factor).astype(out[name].dtype)
    return out
```

```python
from contextlib import ExitStack

import concourse.bass as bass
from concourse import mybir

ALU = mybir.AluOpType
ACT = mybir.ActivationFunctionType
AX = mybir.AxisListType
F32 = mybir.dt.float32
F32R = mybir.dt.float32r
I32 = mybir.dt.int32

P = 128
HEADS = 8
EPS = 1e-5
MASKED = -1000000.0
LOWEST = -3.0e38
RSQRT_MAGIC = 0x5F3759DF
NEWTON = 3
NEWTON_OPS = 4


def block(nc, x, cond, mask, ln_w, ln_b, Wq, bq, Wk, bk, Wv, bv, W_emb, b_emb, ln2_w, ln2_b, W_out, b_out, out):
    B, S, D = x.shape
    TE = cond.shape[1]
    T = S // P
    C = D // P
    DH = D // HEADS
    HC = P // DH
    KE = TE // P
    ME = 2 * D // P
    assert T == 4 and C == 2 and DH == 32 and B >= 4

    x_rows = x.rearrange("b (p t) d -> b p (t d)", t=T)
    out_rows = out.rearrange("b (p t) d -> b p (t d)", t=T)
    mask_rows = mask.rearrange("b s o -> b (s o)")

    with ExitStack() as ctx:
        def sb(name, shape, dt=F32):
            return ctx.enter_context(nc.sbuf_tensor(name, shape, dt))

        def sem(name):
            return ctx.enter_context(nc.semaphore(name))

        bank = [ctx.enter_context(nc.psum_tensor(f"bank{n}", [P, 512], F32)) for n in range(8)]
        K_BANKS = [0, 1]
        QV_BANKS = [4, 5, 2, 3]
        KT_BANKS = [0, 1]
        YT_BANKS = [6, 7]
        QT_BANKS = [4, 5]
        ATT_BANK = 0
        XT_BANKS = [4, 5]
        O_BANKS = [0, 1]
        Y_BANKS = [2, 3, 6, 7]
        COLS_BANK, EMB_T_BANK, EMB_BANK, BIAS_ROW_BANK, BIAS_COL_BANK = 1, 2, 3, 6, 7

        ident = sb("ident", [P, P])
        head_block = sb("head_block", [P, HC, DH])
        ones = sb("ones", [P, P], F32R)
        wk_raw, wk_s = sb("wk_raw", [P, C, D]), sb("wk_s", [P, C, D])
        wk_hi, wk_lo = sb("wk_hi", [P, C, D], F32R), sb("wk_lo", [P, C, D], F32R)
        wqv_raw, wqv_s = sb("wqv_raw", [P, C, 2 * D]), sb("wqv_s", [P, C, 2 * D])
        wqv_hi, wqv_lo = sb("wqv_hi", [P, C, 2 * D], F32R), sb("wqv_lo", [P, C, 2 * D], F32R)
        wo_raw = sb("wo_raw", [P, C, D])
        wo_hi, wo_lo = sb("wo_hi", [P, C, D], F32R), sb("wo_lo", [P, C, D], F32R)
        vectors = [("ln_w", ln_w, C), ("ln_b", ln_b, C), ("bk", bk, C), ("ln2_w", ln2_w, C), ("ln2_b", ln2_b, C),
                   ("b_emb", b_emb, ME)]
        VR = sum(rows for _, _, rows in vectors)
        vec_rows, vec_cols = sb("vec_rows", [VR, P]), sb("vec_cols", [P, VR])
        col, at = {}, 0
        for name, _, rows in vectors:
            col[name] = vec_cols[:, at:at + rows]
            at += rows
        ln_w_col, ln_b_col, bk_in, ln2_w_col, ln2_b_col, b_emb_col = (
            col[name] for name in ("ln_w", "ln_b", "bk", "ln2_w", "ln2_b", "b_emb"))
        bk_col = sb("bk_col", [P, C])
        bqv_in = sb("bqv_in", [1, 2 * D])
        bqv_row = sb("bqv_row", [1, 2 * D])
        bqv_parts = sb("bqv_parts", [P, 2 * D], F32R)
        bo_all = sb("bo_all", [P, D])
        w_emb = sb("w_emb", [P, KE, 2 * D])
        cond_sb, cond_tanh, cond_silu2 = sb("cond_sb", [B, TE]), sb("cond_tanh", [B, TE]), sb("cond_silu2", [B, TE])
        cond_T = sb("cond_T", [P, KE, B])
        emb_T = sb("emb_T", [P, ME, B])
        half_gain, half_shift = sb("half_gain", [P, C, B]), sb("half_shift", [P, C, B])
        mod_scale, mod_shift = sb("mod_scale", [P, C, B]), sb("mod_shift", [P, C, B])
        mask_col = sb("mask_col", [P, B, T])

        x_all = sb("x_all", [P, B, T, D])
        mask_raw, mask_add = sb("mask_raw", [P, S]), sb("mask_add", [P, T, P])
        stats1, mv1, var1, rstd1, newt1 = (sb("stats1", [P, T, 6]), sb("mv1", [P, T, 2]), sb("var1", [P, T]),
                                           sb("rstd1", [P, T]), sb("newt1", [P, T]))
        stats2, mv2, var2, rstd2, newt2 = (sb("stats2", [P, T, 6]), sb("mv2", [P, T, 2]), sb("var2", [P, T]),
                                           sb("rstd2", [P, T]), sb("newt2", [P, T]))
        bits1, bits2 = sb("bits1", [P, T], I32), sb("bits2", [P, T], I32)
        xhat = sb("xhat", [P, T, D])
        xT_hi, xT_lo = sb("xT_hi", [P, C, S], F32R), sb("xT_lo", [P, C, S], F32R)
        k_exp = sb("k_exp", [P, C, S])
        k_max, k_shift, k_bias, k_sum, k_rsum = (sb("k_max", [P, C]), sb("k_shift", [P, C]), sb("k_bias", [P, C]),
                                                 sb("k_sum", [P, C]), sb("k_rsum", [P, C]))
        k_sb, v_sb = sb("k_sb", [P, T, D]), sb("v_sb", [P, T, D])
        q_max = sb("q_max", [P, T, HEADS])
        q_exp = sb("q_exp", [P, T, D])
        qT = sb("qT", [P, C, S])
        att = sb("att", [P, C, P + HC])
        q_rsum = sb("q_rsum", [P, T, HEADS])
        y_sb = sb("y_sb", [P, T, D])
        h_full, h_tanh = sb("h_full", [P, C, S]), sb("h_tanh", [P, C, S])
        h_hi, h_lo = sb("h_hi", [P, C, S], F32R), sb("h_lo", [P, C, S], F32R)

        x_in, mask_in, stored = sem("x_in"), sem("mask_in"), sem("stored")
        wk_in, wqv_in, wo_in, rows_in, bias_rows_in, emb_in, maskcol_in, bo_in = (
            sem("wk_in"), sem("wqv_in"), sem("wo_in"), sem("rows_in"), sem("bias_rows_in"), sem("emb_in"),
            sem("maskcol_in"), sem("bo_in"))
        ident_zero, ident_ready, consts_ready = sem("ident_zero"), sem("ident_ready"), sem("consts_ready")
        cols_mm, cols_ready = sem("cols_mm"), sem("cols_ready")
        w_scaled, w_hi_ready, w_lo_ready = sem("w_scaled"), sem("w_hi_ready"), sem("w_lo_ready")
        bias_mm, bias_step, bias_ready = sem("bias_mm"), sem("bias_step"), sem("bias_ready")
        cond_tanh_ready, cond_silu_ready, cond_T_mm, cond_T_ready, emb_mm, emb_step, mod_ready = (
            sem("cond_tanh_ready"), sem("cond_silu_ready"), sem("cond_T_mm"), sem("cond_T_ready"), sem("emb_mm"),
            sem("emb_step"), sem("mod_ready"))
        xT_mm, k_mm, qv_mm, kT_mm, qT_mm, att_mm, y_mm, yT_mm, o_mm = (
            sem("xT_mm"), sem("k_mm"), sem("qv_mm"), sem("kT_mm"), sem("qT_mm"), sem("att_mm"), sem("y_mm"),
            sem("yT_mm"), sem("o_mm"))
        ln1_step, seed1, xhat_ready, xT_lo_ready = sem("ln1_step"), sem("seed1"), sem("xhat_ready"), sem("xT_lo_ready")
        k_masked, k_step, k_bias_ready = sem("k_masked"), sem("k_step"), sem("k_bias_ready")
        q_max_ready, q_shifted = sem("q_max_ready"), sem("q_shifted")
        rsum_ready, att_ready = sem("rsum_ready"), sem("att_ready")
        y_rsum_ready, y_ready, ln2_step, seed2 = sem("y_rsum_ready"), sem("y_ready"), sem("ln2_step"), sem("seed2")
        h_ready, out_ready = sem("h_ready"), sem("out_ready")
        xT_hi_ready, k_exp_ready, q_exp_ready, v_ready, k_ready, qT_ready, tanh_ready, h_hi_ready = (
            sem("xT_hi_ready"), sem("k_exp_ready"), sem("q_exp_ready"), sem("v_ready"), sem("k_ready"),
            sem("qT_ready"), sem("tanh_ready"), sem("h_hi_ready"))
        mask_ready, newton1_step, rstd1_ready, newton2_step, rstd2_ready, yhat_ready, h_lo_ready, x_biased = (
            sem("mask_ready"), sem("newton1_step"), sem("rstd1_ready"), sem("newton2_step"), sem("rstd2_ready"),
            sem("yhat_ready"), sem("h_lo_ready"), sem("x_biased"))

        passed = sem("passed")
        program = ctx.enter_context(nc.Block())

        def await_then(eng, semaphore, value):
            eng.wait_ge(semaphore, value)
            eng.sem_inc(passed, 1)

        @program.sync
        def _(sp):
            def load_x(n):
                sp.dma_start(x_all[:, bass.ds(n, 1)].rearrange("p a t d -> p (a t d)"),
                             x_rows[bass.ds(n, 1)].rearrange("a p n -> (a p) n")).then_inc(x_in, 16)

            def load_mask(n):
                sp.dma_start(mask_raw[:], mask_rows[bass.ds(n, 1)].broadcast_to([P, S])).then_inc(mask_in, 16)

            def store(n):
                sp.wait_ge(out_ready, n * C + 2 * C)
                sp.dma_start(out_rows[bass.ds(n, 1)].rearrange("a p n -> (a p) n"),
                             x_all[:, bass.ds(n, 1)].rearrange("p a t d -> p (a t d)")).then_inc(stored, 16)

            load_x(0)
            sp.dma_start(wk_raw[:], Wk.rearrange("(c p) n -> p c n", p=P)).then_inc(wk_in, 16)
            load_mask(0)
            sp.dma_start(wqv_raw[:, :, 0:D], Wq.rearrange("(c p) n -> p c n", p=P)).then_inc(wqv_in, 16)
            sp.dma_start(wqv_raw[:, :, D:2 * D], Wv.rearrange("(c p) n -> p c n", p=P)).then_inc(wqv_in, 16)
            sp.wait_ge(x_in, 16)
            load_x(1)
            sp.dma_start(wo_raw[:], W_out.rearrange("(c p) n -> p c n", p=P)).then_inc(wo_in, 16)

            def step(i, more=True, done=True):
                if more:
                    sp.wait_ge(x_in, i * 16 + 32)
                    load_x(i + 2)
                sp.wait_ge(mask_ready, i + 1)
                load_mask(i + 1)
                if done:
                    store(i - 1)

            step(0, done=False)
            with sp.Fori(1, B - 2) as i:
                step(i)
            step(B - 2, more=False)
            store(B - 2)
            half = T // 2
            for b in range(2):
                sp.wait_ge(out_ready, C * B + b + 1)
                sp.dma_start(out_rows[B - 1][:, b * half * D:(b + 1) * half * D],
                             x_all[:, B - 1, b * half:(b + 1) * half].rearrange("p t d -> p (t d)")).then_inc(stored, 16)
            sp.wait_ge(stored, 16 * (B + 1))

        @program.tensor
        def _(pe):
            def split_product(out_ap, stationary, moving, last=None):
                for c in range(C):
                    s_hi, s_lo = stationary(c)
                    m_hi, m_lo = moving(c)
                    nc.tensor.matmul(out_ap, lhsT=s_hi, rhs=m_hi, start=c == 0, stop=False)
                    nc.tensor.matmul(out_ap, lhsT=s_hi, rhs=m_lo, start=False, stop=False)
                    ins = nc.tensor.matmul(out_ap, lhsT=s_lo, rhs=m_hi, start=False, stop=c == C - 1 and last is None)
                if last is not None:
                    ins = nc.tensor.matmul(out_ap, lhsT=last[0], rhs=last[1], start=False, stop=True)
                return ins

            def tokens(t):
                return slice(t * P, (t + 1) * P)

            def channels(c):
                return slice(c * P, (c + 1) * P)

            def transpose_x(n, after_q=True):
                pe.wait_ge(xhat_ready, n * T + T)
                if after_q:
                    pe.wait_ge(qT_ready, n * C)
                for c in range(C):
                    for t in range(T):
                        ins = nc.tensor.transpose(bank[XT_BANKS[c]][:, tokens(t)], xhat[:, t, channels(c)], ident[:])
                    ins.then_inc(xT_mm, 1)

            def project_k(n, first):
                if not first:
                    pe.wait_ge(out_ready, n * C)
                pe.wait_ge(xT_lo_ready, n * C + C)
                for m in range(C):
                    split_product(bank[K_BANKS[m]][:, :],
                                  lambda c: (wk_hi[:, c, channels(m)], wk_lo[:, c, channels(m)]),
                                  lambda c: (xT_hi[:, c, :], xT_lo[:, c, :])).then_inc(k_mm, 1)

            def project_qv(n, t, after_y):
                if after_y and t >= 2:
                    pe.wait_ge(y_ready, n * T - T + t - 1)
                split_product(bank[QV_BANKS[t]][:, :],
                              lambda c: (xT_hi[:, c, tokens(t)], xT_lo[:, c, tokens(t)]),
                              lambda c: (wqv_hi[:, c, :], wqv_lo[:, c, :]),
                              last=(ones[:], bqv_parts[:])).then_inc(qv_mm, 1)

            def transpose_k(n):
                pe.wait_ge(k_exp_ready, n * C + C)
                for t in range(T):
                    for c in range(C):
                        ins = nc.tensor.transpose(bank[KT_BANKS[t // 2]][:, (t % 2) * D + c * P:(t % 2) * D + (c + 1) * P],
                                                  k_exp[:, c, tokens(t)], ident[:])
                    if t % 2 == 1:
                        ins.then_inc(kT_mm, 1)

            def transpose_y(n):
                pe.wait_ge(yhat_ready, n * T + T)
                for c in range(C):
                    for t in range(T):
                        ins = nc.tensor.transpose(bank[YT_BANKS[c]][:, tokens(t)], y_sb[:, t, channels(c)], ident[:])
                    ins.then_inc(yT_mm, 1)

            def transpose_q(n):
                pe.wait_ge(q_exp_ready, n * T + T)
                pe.wait_ge(v_ready, n * T + 2)
                for c in range(C):
                    for t in range(T):
                        ins = nc.tensor.transpose(bank[QT_BANKS[c]][:, tokens(t)], q_exp[:, t, channels(c)], ident[:])
                    ins.then_inc(qT_mm, 1)

            def attend_k_v(n):
                pe.wait_ge(k_ready, n * 2 + 2)
                pe.wait_ge(v_ready, n * T + T)
                for c in range(C):
                    for t in range(T):
                        ins = nc.tensor.matmul(bank[ATT_BANK][:, channels(c)], lhsT=k_sb[:, t, channels(c)],
                                               rhs=v_sb[:, t, channels(c)], start=t == 0, stop=t == T - 1)
                ins.then_inc(att_mm, 1)

            def attend_q(n):
                pe.wait_ge(qT_ready, n * C + C)
                pe.wait_ge(att_ready, n * C + C)
                for t in range(T):
                    for c in range(C):
                        ins = nc.tensor.matmul(bank[Y_BANKS[t]][:, c * (P + HC):(c + 1) * (P + HC)],
                                               lhsT=qT[:, c, tokens(t)], rhs=att[:, c, :], start=True, stop=True)
                    ins.then_inc(y_mm, 1)

            def project_out(n, at_end=False):
                pe.wait_ge(h_lo_ready, n * C + C)
                if at_end:
                    pe.wait_ge(out_ready, n * C + C)
                else:
                    pe.wait_ge(att_ready, n * C + 2 * C)
                for t in range(T):
                    ins = split_product(bank[O_BANKS[t // 2]][:, (t % 2) * D:(t % 2 + 1) * D],
                                        lambda c: (h_hi[:, c, tokens(t)], h_lo[:, c, tokens(t)]),
                                        lambda c: (wo_hi[:, c, :], wo_lo[:, c, :]))
                    if t % 2 == 1:
                        ins.then_inc(o_mm, 1)

            def bias_products():
                pe.wait_ge(wqv_in, 32)
                for m in range(C):
                    for c in range(C):
                        nc.tensor.matmul(bank[BIAS_COL_BANK][:, m:m + 1], lhsT=wk_raw[:, c, channels(m)],
                                         rhs=ln_b_col[:, c:c + 1], start=c == 0, stop=c == C - 1)
                for c in range(C):
                    ins = nc.tensor.matmul(bank[BIAS_ROW_BANK][0:1, :], lhsT=ln_b_col[:, c:c + 1],
                                           rhs=wqv_raw[:, c, :], start=c == 0, stop=c == C - 1)
                ins.then_inc(bias_mm, 1)

            def embed():
                pe.wait_ge(cond_silu_ready, 1)
                for k in range(KE):
                    ins = nc.tensor.transpose(bank[EMB_T_BANK][:, k * B:(k + 1) * B], cond_silu2[:, k * P:(k + 1) * P],
                                              ident[0:B, 0:B])
                ins.then_inc(cond_T_mm, 1)
                pe.wait_ge(cond_T_ready, 1)
                for m in range(ME):
                    for k in range(KE):
                        ins = nc.tensor.matmul(bank[EMB_BANK][:, m * B:(m + 1) * B], lhsT=w_emb[:, k, m * P:(m + 1) * P],
                                               rhs=cond_T[:, k, :], start=k == 0, stop=k == KE - 1)
                ins.then_inc(emb_mm, 1)

            def step(i, first=False, last=False):
                project_k(i, first)
                for t in range(T):
                    if not (first and t == 2):
                        project_qv(i, t, not first)
                    else:
                        pe.wait_ge(emb_step, 1)
                        project_qv(i, t, False)
                transpose_k(i)
                if not first:
                    transpose_y(i - 1)
                transpose_q(i)
                attend_k_v(i)
                if not last:
                    transpose_x(i + 1)
                if not first:
                    project_out(i - 1)
                attend_q(i)

            pe.wait_ge(ident_ready, 1)
            pe.wait_ge(rows_in, 16 * len(vectors))
            nc.tensor.transpose(bank[COLS_BANK][:, 0:VR], vec_rows[:], ident[0:VR, 0:VR]).then_inc(cols_mm, 1)
            transpose_x(0, after_q=False)
            pe.wait_ge(cols_ready, 1)
            pe.wait_ge(wk_in, 16)
            bias_products()
            embed()
            pe.wait_ge(w_lo_ready, 2)
            pe.wait_ge(bias_ready, 2)
            step(0, first=True)
            with pe.Fori(1, B - 1) as i:
                step(i)
            step(B - 1, last=True)
            transpose_y(B - 1)
            project_out(B - 1, at_end=True)

        @program.vector
        def _(dve):
            def seed_rsqrt(var, bits, rstd, mv, step_sem, seed_sem, n, before):
                dve.wait_ge(step_sem, n * 4 + before)
                nc.vector.tensor_scalar(var[:], mv[:, :, 1], EPS, None, ALU.add).then_inc(step_sem, 1)
                dve.wait_ge(step_sem, n * 4 + before + 1)
                nc.vector.tensor_scalar(bits[:], var[:].bitcast(I32), 1, None, ALU.logical_shift_right).then_inc(step_sem, 1)
                dve.wait_ge(step_sem, n * 4 + before + 2)
                nc.vector.tensor_scalar(rstd[:].bitcast(I32), bits[:], -1.0, float(RSQRT_MAGIC), ALU.mult,
                                        ALU.add).then_inc(seed_sem, 1)

            def x_statistics(n):
                dve.wait_ge(x_in, n * 16 + 16)
                for t in range(T):
                    ins = nc.vector.bn_stats(stats1[:, t, :], x_all[:, bass.ds(n, 1), t, :].rearrange("p a d -> p (a d)"))
                ins.then_inc(ln1_step, 1)
                await_then(dve, ln1_step, n * 4 + 1)
                for t in range(T):
                    ins = nc.vector.bn_aggr(mv1[:, t, :], stats1[:, t, :])
                ins.then_inc(ln1_step, 1)
                seed_rsqrt(var1, bits1, rstd1, mv1, ln1_step, seed1, n, 2)

            def normalise_x(n):
                dve.wait_ge(rstd1_ready, n + 1)
                for t in range(T):
                    nc.vector.tensor_scalar(xhat[:, t, :], x_all[:, bass.ds(n, 1), t, :].rearrange("p a d -> p (a d)"),
                                            mv1[:, t, 0:1], rstd1[:, t:t + 1], ALU.subtract, ALU.mult).then_inc(xhat_ready, 1)

            def rest_of_xT(n):
                for c in range(C):
                    dve.wait_ge(xT_hi_ready, n * C + c + 1)
                    nc.vector.tensor_tensor(xT_lo[:, c, :], bank[XT_BANKS[c]][:, :], xT_hi[:, c, :].bitcast(F32),
                                            ALU.subtract).then_inc(xT_lo_ready, 1)

            def mask_k(n):
                dve.wait_ge(mask_ready, n + 1)
                for c in range(C):
                    await_then(dve, k_mm, n * C + c + 1)
                    nc.vector.tensor_tensor_reduce(k_exp[:, c, :], bank[K_BANKS[c]][:, :],
                                                   mask_add[:].rearrange("p t s -> p (t s)"), 1.0, LOWEST,
                                                   ALU.add, ALU.max, k_max[:, c:c + 1]).then_inc(k_masked, 1)
                dve.wait_ge(k_masked, n * C + C)
                nc.vector.tensor_tensor(k_shift[:], k_max[:], bk_col[:], ALU.add).then_inc(k_step, 1)
                dve.wait_ge(k_step, n + 1)
                nc.vector.tensor_tensor(k_bias[:], bk_col[:], k_shift[:], ALU.subtract).then_inc(k_bias_ready, 1)

            def shift_q(n, t):
                q = bank[QV_BANKS[t]][:, 0:D].rearrange("p (h d) -> p h d", h=HEADS)
                dve.wait_ge(qv_mm, n * T + t + 1)
                nc.vector.tensor_reduce(q_max[:, t, :], q, AX.X, ALU.max).then_inc(q_max_ready, 1)
                dve.wait_ge(q_max_ready, n * T + t + 1)
                nc.vector.tensor_tensor(q_exp[:, t, :].rearrange("p (h d) -> p h d", h=HEADS), q,
                                        q_max[:, t, :].unsqueeze(2).to_broadcast([P, HEADS, DH]),
                                        ALU.subtract).then_inc(q_shifted, 1)

            def normalise_att(n):
                dve.wait_ge(k_exp_ready, n * C + C)
                nc.vector.reciprocal(k_rsum[:], k_sum[:]).then_inc(rsum_ready, 1)
                dve.wait_ge(rsum_ready, n + 1)
                dve.wait_ge(att_mm, n + 1)
                for c in range(C):
                    nc.vector.scalar_tensor_tensor(out=att[:, c, 0:P], in0=bank[ATT_BANK][:, c * P:(c + 1) * P],
                                                   scalar=k_rsum[:, c:c + 1], in1=head_block[:].rearrange("p h d -> p (h d)"),
                                                   op0=ALU.mult, op1=ALU.mult).then_inc(att_ready, 1)

            def normalise_y(n):
                for t in range(T):
                    y = bank[Y_BANKS[t]][:, 0:C * (P + HC)].rearrange("p (c n) -> p c n", c=C)
                    dve.wait_ge(y_mm, n * T + t + 1)
                    nc.vector.reciprocal(q_rsum[:, t, :].rearrange("p (c h) -> p c h", c=C), y[:, :, P:P + HC]).then_inc(y_rsum_ready, 1)
                    dve.wait_ge(y_rsum_ready, n * T + t + 1)
                    nc.vector.tensor_tensor(y_sb[:, t, :].rearrange("p (c h d) -> p c h d", c=C, h=HC),
                                            y[:, :, 0:P].rearrange("p c (h d) -> p c h d", h=HC),
                                            q_rsum[:, t, :].rearrange("p (c h) -> p c h", c=C).unsqueeze(3).to_broadcast([P, C, HC, DH]),
                                            ALU.mult).then_inc(y_ready, 1)

            def y_statistics(n):
                for t in range(T):
                    dve.wait_ge(y_ready, n * T + t + 1)
                    ins = nc.vector.bn_stats(stats2[:, t, :], y_sb[:, t, :])
                ins.then_inc(ln2_step, 1)
                await_then(dve, ln2_step, n * 4 + 1)
                for t in range(T):
                    ins = nc.vector.bn_aggr(mv2[:, t, :], stats2[:, t, :])
                ins.then_inc(ln2_step, 1)
                seed_rsqrt(var2, bits2, rstd2, mv2, ln2_step, seed2, n, 2)

            def gate_h(n):
                for c in range(C):
                    dve.wait_ge(tanh_ready, n * C + c + 1)
                    nc.vector.scalar_tensor_tensor(out=h_full[:, c, :], in0=h_tanh[:, c, :], scalar=1.0, in1=h_full[:, c, :],
                                                   op0=ALU.add, op1=ALU.mult).then_inc(h_ready, 1)

            def add_out(n):
                dve.wait_ge(x_biased, n + 1)
                for b in range(2):
                    dve.wait_ge(o_mm, n * 2 + b + 1)
                    rows = x_all[:, bass.ds(n, 1), 2 * b:2 * b + 2, :].rearrange("p a t d -> p (a t d)")
                    nc.vector.tensor_tensor(rows, bank[O_BANKS[b]][:, :], rows, ALU.add).then_inc(out_ready, 1)

            def split_weights():
                def rest(lo, full, hi, order):
                    dve.wait_ge(w_hi_ready, order)
                    nc.vector.tensor_tensor(lo[:], full[:], hi[:].bitcast(F32), ALU.subtract).then_inc(w_lo_ready, 1)

                dve.wait_ge(cols_mm, 1)
                nc.vector.tensor_copy(vec_cols[:], bank[COLS_BANK][:, 0:VR]).then_inc(cols_ready, 1)
                dve.wait_ge(cols_ready, 1)
                dve.wait_ge(wk_in, 16)
                for c in range(C):
                    ins = nc.vector.tensor_scalar(wk_s[:, c, :], wk_raw[:, c, :], ln_w_col[:, c:c + 1], None, ALU.mult)
                ins.then_inc(w_scaled, 1)
                dve.wait_ge(wqv_in, 32)
                for c in range(C):
                    ins = nc.vector.tensor_scalar(wqv_s[:, c, :], wqv_raw[:, c, :], ln_w_col[:, c:c + 1], None, ALU.mult)
                ins.then_inc(w_scaled, 1)
                rest(wk_lo, wk_s, wk_hi, 1)
                rest(wqv_lo, wqv_s, wqv_hi, 2)
                dve.wait_ge(wo_in, 16)
                rest(wo_lo, wo_raw, wo_hi, 3)

            def biases():
                dve.wait_ge(bias_mm, 1)
                dve.wait_ge(bias_rows_in, 32)
                dve.wait_ge(consts_ready, 1)
                nc.vector.tensor_tensor(bk_col[:], bank[BIAS_COL_BANK][:, 0:C], bk_in[:], ALU.add).then_inc(bias_ready, 1)
                nc.vector.tensor_tensor(bqv_row[:], bank[BIAS_ROW_BANK][0:1, :], bqv_in[:], ALU.add).then_inc(bias_step, 1)
                dve.wait_ge(bias_step, 1)
                nc.vector.tensor_copy(bqv_parts[0:1, :], bqv_row[:]).then_inc(bias_step, 1)
                dve.wait_ge(bias_step, 2)
                nc.vector.tensor_tensor(bqv_parts[32:33, :], bqv_row[:], bqv_parts[0:1, :].bitcast(F32),
                                        ALU.subtract).then_inc(bias_ready, 1)

            def silu_cond():
                dve.wait_ge(cond_tanh_ready, 1)
                nc.vector.scalar_tensor_tensor(out=cond_silu2[:], in0=cond_tanh[:], scalar=1.0, in1=cond_sb[:],
                                               op0=ALU.add, op1=ALU.mult).then_inc(cond_silu_ready, 1)
                dve.wait_ge(cond_T_mm, 1)
                nc.vector.tensor_copy(cond_T[:].rearrange("p k b -> p (k b)"), bank[EMB_T_BANK][:, 0:KE * B]).then_inc(cond_T_ready, 1)

            def modulation():
                dve.wait_ge(emb_mm, 1)
                for m in range(ME):
                    ins = nc.vector.tensor_scalar(emb_T[:, m, :], bank[EMB_BANK][:, m * B:(m + 1) * B], 0.5, b_emb_col[:, m:m + 1],
                                                  ALU.mult, ALU.add)
                ins.then_inc(emb_step, 1)
                dve.wait_ge(emb_step, 1)
                nc.vector.tensor_scalar(half_gain[:], emb_T[:, 0:C, :], 1.0, 0.5, ALU.add, ALU.mult)
                nc.vector.tensor_scalar(half_shift[:], emb_T[:, C:2 * C, :], 0.5, None, ALU.mult).then_inc(emb_step, 1)
                dve.wait_ge(emb_step, 2)
                for c in range(C):
                    nc.vector.tensor_scalar(mod_scale[:, c, :], half_gain[:, c, :], ln2_w_col[:, c:c + 1], None, ALU.mult)
                    ins = nc.vector.scalar_tensor_tensor(out=mod_shift[:, c, :], in0=half_gain[:, c, :], scalar=ln2_b_col[:, c:c + 1],
                                                         in1=half_shift[:, c, :], op0=ALU.mult, op1=ALU.add)
                ins.then_inc(mod_ready, 1)

            def step(i, first=False, last=False):
                if not first:
                    normalise_y(i - 1)
                    y_statistics(i - 1)
                mask_k(i)
                for t in range(T):
                    shift_q(i, t)
                if not last:
                    x_statistics(i + 1)
                if not first:
                    gate_h(i - 1)
                if not last:
                    normalise_x(i + 1)
                normalise_att(i)
                if not last:
                    rest_of_xT(i + 1)
                if not first:
                    add_out(i - 1)

            dve.sem_inc(out_ready, C)
            x_statistics(0)
            split_weights()
            normalise_x(0)
            silu_cond()
            biases()
            rest_of_xT(0)
            modulation()
            step(0, first=True)
            with dve.Fori(1, B - 1) as i:
                step(i)
            step(B - 1, last=True)
            normalise_y(B - 1)
            y_statistics(B - 1)
            gate_h(B - 1)
            add_out(B - 1)

        @program.scalar
        def _(act):
            def split_hi_x(n):
                for c in range(C):
                    act.wait_ge(xT_mm, n * C + c + 1)
                    nc.scalar.activation(xT_hi[:, c, :], bank[XT_BANKS[c]][:, :], ACT.Copy).then_inc(xT_hi_ready, 1)

            def exp_k(n):
                act.wait_ge(k_bias_ready, n + 1)
                for c in range(C):
                    nc.scalar.activation(k_exp[:, c, :], k_exp[:, c, :], ACT.Exp, bias=k_bias[:, c:c + 1],
                                         accum_out=k_sum[:, c:c + 1]).then_inc(k_exp_ready, 1)

            def exp_q_and_mask_v(n, t):
                act.wait_ge(q_shifted, n * T + t + 1)
                nc.scalar.activation(q_exp[:, t, :], q_exp[:, t, :], ACT.Exp).then_inc(q_exp_ready, 1)
                nc.scalar.activation(v_sb[:, t, :], bank[QV_BANKS[t]][:, D:2 * D], ACT.Copy,
                                     scale=mask_col[:, bass.ds(n, 1), t:t + 1].rearrange("p a t -> p (a t)")).then_inc(v_ready, 1)

            def copy_k(n):
                for b in range(2):
                    act.wait_ge(kT_mm, n * 2 + b + 1)
                    nc.scalar.activation(k_sb[:, 2 * b:2 * b + 2, :].rearrange("p t d -> p (t d)"), bank[KT_BANKS[b]][:, :],
                                         ACT.Copy).then_inc(k_ready, 1)

            def copy_qT(n):
                for c in range(C):
                    act.wait_ge(qT_mm, n * C + c + 1)
                    nc.scalar.activation(qT[:, c, :], bank[QT_BANKS[c]][:, :], ACT.Copy).then_inc(qT_ready, 1)

            def modulate(n):
                for c in range(C):
                    scale = mod_scale[:, c, bass.ds(n, 1)]
                    shift = mod_shift[:, c, bass.ds(n, 1)]
                    act.wait_ge(yT_mm, n * C + c + 1)
                    nc.scalar.activation(h_full[:, c, :], bank[YT_BANKS[c]][:, :], ACT.Identity, scale=scale, bias=shift)
                    nc.scalar.activation(h_tanh[:, c, :], bank[YT_BANKS[c]][:, :], ACT.Tanh, scale=scale, bias=shift).then_inc(tanh_ready, 1)

            def split_hi_h(n):
                for c in range(C):
                    act.wait_ge(h_ready, n * C + c + 1)
                    nc.scalar.activation(h_hi[:, c, :], h_full[:, c, :], ACT.Copy).then_inc(h_hi_ready, 1)

            def step(i, first=False, last=False):
                exp_k(i)
                for t in range(T):
                    exp_q_and_mask_v(i, t)
                copy_k(i)
                if not first:
                    modulate(i - 1)
                copy_qT(i)
                if not first:
                    split_hi_h(i - 1)
                if not last:
                    split_hi_x(i + 1)

            row = 0
            for _, vector, rows in vectors:
                act.dma_start(vec_rows[row:row + rows, :], vector.rearrange("(c p) -> c p", p=P)).then_inc(rows_in, 16)
                row += rows
            act.dma_start(cond_sb[:], cond).then_inc(emb_in, 16)
            act.dma_start(bqv_in[:, 0:D], bq.rearrange("(a d) -> a d", a=1)).then_inc(bias_rows_in, 16)
            act.dma_start(bqv_in[:, D:2 * D], bv.rearrange("(a d) -> a d", a=1)).then_inc(bias_rows_in, 16)
            act.dma_start(w_emb[:], W_emb.rearrange("(k p) n -> p k n", p=P)).then_inc(emb_in, 16)
            act.dma_start(mask_col[:], mask.rearrange("b (p t) o -> p b (t o)", t=T)).then_inc(maskcol_in, 16)
            act.dma_start(bo_all[:], b_out.rearrange("(a d) -> a d", a=1).broadcast_to([P, D])).then_inc(bo_in, 16)
            act.wait_ge(emb_in, 32)
            nc.scalar.activation(cond_tanh[:], cond_sb[:], ACT.Tanh, scale=0.5).then_inc(cond_tanh_ready, 1)
            act.wait_ge(w_scaled, 1)
            nc.scalar.activation(wk_hi[:], wk_s[:], ACT.Copy).then_inc(w_hi_ready, 1)
            act.wait_ge(w_scaled, 2)
            nc.scalar.activation(wqv_hi[:], wqv_s[:], ACT.Copy).then_inc(w_hi_ready, 1)
            act.wait_ge(wo_in, 16)
            nc.scalar.activation(wo_hi[:], wo_raw[:], ACT.Copy).then_inc(w_hi_ready, 1)
            split_hi_x(0)
            act.wait_ge(maskcol_in, 16)
            act.wait_ge(mod_ready, 1)
            step(0, first=True)
            with act.Fori(1, B - 1) as i:
                step(i)
            step(B - 1, last=True)
            modulate(B - 1)
            split_hi_h(B - 1)

        @program.gpsimd
        def _(pool):
            def prepare_mask(n, again=True):
                pool.wait_ge(mask_in, n * 16 + 16)
                if again:
                    await_then(pool, k_masked, n * C)
                nc.gpsimd.tensor_scalar(mask_add[:], mask_raw[:].rearrange("p (s t) -> p t s", t=T), -1.0, -MASKED,
                                        ALU.add, ALU.mult).then_inc(mask_ready, 1)

            def newton(n, var, rstd, work, seed_sem, step_sem, ready_sem):
                steps = NEWTON * NEWTON_OPS - 1
                pool.wait_ge(seed_sem, n + 1)
                for s in range(NEWTON):
                    at = s * NEWTON_OPS
                    if s:
                        pool.wait_ge(step_sem, n * steps + at)
                    nc.gpsimd.tensor_tensor(work[:], rstd[:], rstd[:], ALU.mult).then_inc(step_sem, 1)
                    pool.wait_ge(step_sem, n * steps + at + 1)
                    nc.gpsimd.tensor_tensor(work[:], work[:], var[:], ALU.mult).then_inc(step_sem, 1)
                    await_then(pool, step_sem, n * steps + at + 2)
                    nc.gpsimd.tensor_scalar(work[:], work[:], -0.5, 1.5, ALU.mult, ALU.add).then_inc(step_sem, 1)
                    pool.wait_ge(step_sem, n * steps + at + 3)
                    ins = nc.gpsimd.tensor_tensor(rstd[:], rstd[:], work[:], ALU.mult)
                    ins.then_inc(step_sem if s < NEWTON - 1 else ready_sem, 1)

            def newton_x(n):
                newton(n, var1, rstd1, newt1, seed1, newton1_step, rstd1_ready)

            def normalise_y(n):
                newton(n, var2, rstd2, newt2, seed2, newton2_step, rstd2_ready)
                await_then(pool, rstd2_ready, n + 1)
                for t in range(T):
                    nc.gpsimd.tensor_scalar(y_sb[:, t, :], y_sb[:, t, :], mv2[:, t, 0:1], rstd2[:, t:t + 1],
                                            ALU.subtract, ALU.mult).then_inc(yhat_ready, 1)

            def bias_x(n):
                pool.wait_ge(xhat_ready, n * T + T)
                rows = x_all[:, bass.ds(n, 1), :, :].rearrange("p a t d -> p (a t) d")
                nc.gpsimd.tensor_tensor(rows, rows, bo_all[:].unsqueeze(1).to_broadcast([P, T, D]), ALU.add).then_inc(x_biased, 1)

            def rest_of_h(n):
                for c in range(C):
                    pool.wait_ge(h_hi_ready, n * C + c + 1)
                    nc.gpsimd.tensor_tensor(h_lo[:, c, :], h_full[:, c, :], h_hi[:, c, :].bitcast(F32),
                                            ALU.subtract).then_inc(h_lo_ready, 1)

            def step(i, first=False, last=False):
                if not first:
                    normalise_y(i - 1)
                if not last:
                    prepare_mask(i + 1)
                    newton_x(i + 1)
                if not first:
                    rest_of_h(i - 1)
                if not last:
                    bias_x(i + 1)

            nc.gpsimd.memset(ident[:], 0.0).then_inc(ident_zero, 1)
            pool.wait_ge(ident_zero, 1)
            nc.gpsimd.affine_select(out=ident[:], in_=ident[:], compare_op=ALU.not_equal, fill=1.0, base=0,
                                    pattern=[[-1, P]], channel_multiplier=1).then_inc(ident_ready, 1)
            nc.gpsimd.memset(ones[:].bitcast(F32), 1.0)
            nc.gpsimd.memset(bqv_parts[:].bitcast(F32), 0.0)
            nc.gpsimd.memset(head_block[:], 0.0)
            nc.gpsimd.memset(att[:], 0.0).then_inc(ident_zero, 1)
            pool.wait_ge(ident_zero, 2)
            for h in range(HC):
                nc.gpsimd.memset(head_block[h * DH:(h + 1) * DH, h, :], 1.0)
                ins = nc.gpsimd.memset(att[h * DH:(h + 1) * DH, :, P + h:P + h + 1], 1.0)
            ins.then_inc(consts_ready, 1)
            pool.wait_ge(consts_ready, 1)
            newton_x(0)
            prepare_mask(0, again=False)
            pool.wait_ge(bo_in, 16)
            bias_x(0)
            step(0, first=True)
            with pool.Fori(1, B - 1) as i:
                step(i)
            step(B - 1, last=True)
            normalise_y(B - 1)
            rest_of_h(B - 1)


_INS = ["x", "cond_2048", "mask_BxSx1_fk1", "L0_cond_ln_w", "L0_cond_ln_b", "L0_cond_Wq", "L0_cond_bq", "L0_cond_Wk",
        "L0_cond_bk", "L0_cond_Wv", "L0_cond_bv", "L0_cond_W_emb", "L0_cond_b_emb", "L0_cond_ln2_w", "L0_cond_ln2_b",
        "L0_cond_W_out", "L0_cond_b_out"]


def kernel(**inputs):
    import numpy as np
    import concourse.bacc as bacc
    from concourse.bass_utils import run_bass_kernel_spmd

    nc = bacc.Bacc("TRN2", target_bir_lowering=False, num_devices=1)
    arrays, args = {}, []
    for name in _INS:
        a = np.ascontiguousarray(inputs[name])
        arrays[f"in_{name}"] = a
        args.append(nc.dram_tensor(f"in_{name}", a.shape, mybir.dt.from_np(a.dtype), kind="ExternalInput").ap())
    shape = np.asarray(inputs["x"]).shape
    out = nc.dram_tensor("out", shape, F32, kind="ExternalOutput").ap()
    block(nc, *args, out)
    r = run_bass_kernel_spmd(nc, [arrays], core_ids=[0])
    return r.results[0]["out"]
```

```python
from contextlib import ExitStack

import concourse.bass as bass
from concourse import mybir

ALU = mybir.AluOpType
ACT = mybir.ActivationFunctionType
AX = mybir.AxisListType
F32 = mybir.dt.float32
F32R = mybir.dt.float32r
I32 = mybir.dt.int32

P = 128
HEADS = 8
EPS = 1e-5
MASKED = -1000000.0
LOWEST = -3.0e38
RSQRT_MAGIC = 0x5F3759DF
NEWTON = 3
NEWTON_OPS = 4


def block(nc, x, cond, mask, ln_w, ln_b, Wq, bq, Wk, bk, Wv, bv, W_emb, b_emb, ln2_w, ln2_b, W_out, b_out, out):
    B, S, D = x.shape
    TE = cond.shape[1]
    T = S // P
    C = D // P
    DH = D // HEADS
    HC = P // DH
    KE = TE // P
    ME = 2 * D // P
    assert T == 4 and C == 2 and DH == 32 and B >= 4

    x_rows = x.rearrange("b (p t) d -> b p (t d)", t=T)
    out_rows = out.rearrange("b (p t) d -> b p (t d)", t=T)
    mask_rows = mask.rearrange("b s o -> b (s o)")

    with ExitStack() as ctx:
        def sb(name, shape, dt=F32):
            return ctx.enter_context(nc.sbuf_tensor(name, shape, dt))

        def sem(name):
            return ctx.enter_context(nc.semaphore(name))

        bank = [ctx.enter_context(nc.psum_tensor(f"bank{n}", [P, 512], F32)) for n in range(8)]
        K_BANKS = [0, 1]
        QV_BANKS = [2, 3, 4, 5]
        KT_BANKS = [0, 1]
        YT_BANKS = [6, 7]
        QT_BANKS = [2, 3]
        ATT_BANK = 0
        XT_BANKS = [4, 5]
        O_BANKS = [0, 1]
        Y_BANKS = [1, 2, 3, 6]
        COLS_BANK, BIAS_ROW_BANK, BIAS_COL_BANK = 0, 1, 2
        EMB_T_BANK, EMB_BANK = 6, 7

        ident = sb("ident", [P, P])
        head_block = sb("head_block", [P, HC, DH])
        ones = sb("ones", [P, P], F32R)
        wk_raw, wk_s = sb("wk_raw", [P, C, D]), sb("wk_s", [P, C, D])
        wk_hi, wk_lo = sb("wk_hi", [P, C, D], F32R), sb("wk_lo", [P, C, D], F32R)
        wqv_raw, wqv_s = sb("wqv_raw", [P, C, 2 * D]), sb("wqv_s", [P, C, 2 * D])
        wqv_hi, wqv_lo = sb("wqv_hi", [P, C, 2 * D], F32R), sb("wqv_lo", [P, C, 2 * D], F32R)
        wo_raw = sb("wo_raw", [P, C, D])
        wo_hi, wo_lo = sb("wo_hi", [P, C, D], F32R), sb("wo_lo", [P, C, D], F32R)
        vectors = [("ln_w", ln_w, C), ("ln_b", ln_b, C), ("bk", bk, C), ("ln2_w", ln2_w, C), ("ln2_b", ln2_b, C),
                   ("b_emb", b_emb, ME)]
        VR = sum(rows for _, _, rows in vectors)
        vec_rows, vec_cols = sb("vec_rows", [VR, P]), sb("vec_cols", [P, VR])
        col, at = {}, 0
        for name, _, rows in vectors:
            col[name] = vec_cols[:, at:at + rows]
            at += rows
        ln_w_col, ln_b_col, bk_in, ln2_w_col, ln2_b_col, b_emb_col = (
            col[name] for name in ("ln_w", "ln_b", "bk", "ln2_w", "ln2_b", "b_emb"))
        bk_col = sb("bk_col", [P, C])
        bqv_in = sb("bqv_in", [1, 2 * D])
        bqv_row = sb("bqv_row", [1, 2 * D])
        bqv_parts = sb("bqv_parts", [P, 2 * D], F32R)
        bo_all = sb("bo_all", [P, D])
        w_emb = sb("w_emb", [P, KE, 2 * D])
        cond_sb, cond_tanh, cond_silu2 = sb("cond_sb", [B, TE]), sb("cond_tanh", [B, TE]), sb("cond_silu2", [B, TE])
        cond_T = sb("cond_T", [P, KE, B])
        emb_T = sb("emb_T", [P, ME, B])
        half_gain, half_shift = sb("half_gain", [P, C, B]), sb("half_shift", [P, C, B])
        mod_scale, mod_shift = sb("mod_scale", [P, C, B]), sb("mod_shift", [P, C, B])
        mask_col = sb("mask_col", [P, B, T])

        x_all = sb("x_all", [P, B, T, D])
        mask_raw, mask_add = sb("mask_raw", [P, S]), sb("mask_add", [P, T, P])
        stats1, mv1, var1, rstd1, newt1 = (sb("stats1", [P, T, 6]), sb("mv1", [P, T, 2]), sb("var1", [P, T]),
                                           sb("rstd1", [P, T]), sb("newt1", [P, T]))
        stats2, mv2, var2, rstd2, newt2 = (sb("stats2", [P, T, 6]), sb("mv2", [P, T, 2]), sb("var2", [P, T]),
                                           sb("rstd2", [P, T]), sb("newt2", [P, T]))
        bits1, bits2 = sb("bits1", [P, T], I32), sb("bits2", [P, T], I32)
        xhat = sb("xhat", [P, T, D])
        xT_hi, xT_lo = sb("xT_hi", [P, C, S], F32R), sb("xT_lo", [P, C, S], F32R)
        k_exp = sb("k_exp", [P, C, S])
        k_max, k_shift, k_bias, k_sum, k_rsum = (sb("k_max", [P, C]), sb("k_shift", [P, C]), sb("k_bias", [P, C]),
                                                 sb("k_sum", [P, C]), sb("k_rsum", [P, C]))
        k_sb, v_sb = sb("k_sb", [P, T, D]), sb("v_sb", [P, T, D])
        q_max = sb("q_max", [P, T, HEADS])
        q_exp = sb("q_exp", [P, T, D])
        qT = sb("qT", [P, C, S])
        att = sb("att", [P, C, P + HC])
        q_rsum = sb("q_rsum", [P, T, HEADS])
        y_sb = sb("y_sb", [P, T, D])
        mean_rstd, y_bias = sb("mean_rstd", [P, T]), sb("y_bias", [P, T])
        h_full, h_tanh = sb("h_full", [P, C, S]), sb("h_tanh", [P, C, S])
        h_hi, h_lo = sb("h_hi", [P, C, S], F32R), sb("h_lo", [P, C, S], F32R)

        x_in, mask_in, stored = sem("x_in"), sem("mask_in"), sem("stored")
        cond_in, wk_in, wqv_in, wo_in, rows_in, bias_rows_in, emb_in, maskcol_in, bo_in = (
            sem("cond_in"), sem("wk_in"), sem("wqv_in"), sem("wo_in"), sem("rows_in"), sem("bias_rows_in"), sem("emb_in"),
            sem("maskcol_in"), sem("bo_in"))
        ident_zero, ident_ready, consts_ready = sem("ident_zero"), sem("ident_ready"), sem("consts_ready")
        cols_mm, cols_ready = sem("cols_mm"), sem("cols_ready")
        w_scaled, w_hi_ready, w_lo_ready = sem("w_scaled"), sem("w_hi_ready"), sem("w_lo_ready")
        bias_mm, bias_step, bias_ready = sem("bias_mm"), sem("bias_step"), sem("bias_ready")
        cond_tanh_ready, cond_silu_ready, cond_T_mm, cond_T_ready, emb_mm, emb_step, mod_ready = (
            sem("cond_tanh_ready"), sem("cond_silu_ready"), sem("cond_T_mm"), sem("cond_T_ready"), sem("emb_mm"),
            sem("emb_step"), sem("mod_ready"))
        xT_mm, k_mm, qv_mm, kT_mm, qT_mm, att_mm, y_mm, yT_mm, o_mm = (
            sem("xT_mm"), sem("k_mm"), sem("qv_mm"), sem("kT_mm"), sem("qT_mm"), sem("att_mm"), sem("y_mm"),
            sem("yT_mm"), sem("o_mm"))
        ln1_step, seed1, xhat_ready, xT_lo_ready = sem("ln1_step"), sem("seed1"), sem("xhat_ready"), sem("xT_lo_ready")
        k_masked, k_step, k_bias_ready = sem("k_masked"), sem("k_step"), sem("k_bias_ready")
        q_max_ready, q_shifted = sem("q_max_ready"), sem("q_shifted")
        rsum_ready, att_ready = sem("rsum_ready"), sem("att_ready")
        y_rsum_ready, y_ready, ln2_step, seed2 = sem("y_rsum_ready"), sem("y_ready"), sem("ln2_step"), sem("seed2")
        h_ready, out_ready = sem("h_ready"), sem("out_ready")
        xT_hi_ready, k_exp_ready, q_exp_ready, v_ready, k_ready, qT_ready, tanh_ready, h_hi_ready = (
            sem("xT_hi_ready"), sem("k_exp_ready"), sem("q_exp_ready"), sem("v_ready"), sem("k_ready"),
            sem("qT_ready"), sem("tanh_ready"), sem("h_hi_ready"))
        mask_ready, newton1_step, rstd1_ready, newton2_step, rstd2_ready, yhat_ready, h_lo_ready, x_biased = (
            sem("mask_ready"), sem("newton1_step"), sem("rstd1_ready"), sem("newton2_step"), sem("rstd2_ready"),
            sem("yhat_ready"), sem("h_lo_ready"), sem("x_biased"))
        mean_rstd_ready, y_bias_ready = sem("mean_rstd_ready"), sem("y_bias_ready")

        passed = sem("passed")
        program = ctx.enter_context(nc.Block())

        def await_then(eng, semaphore, value):
            eng.wait_ge(semaphore, value)
            eng.sem_inc(passed, 1)

        @program.sync
        def _(sp):
            def load_x(n):
                sp.dma_start(x_all[:, bass.ds(n, 1)].rearrange("p a t d -> p (a t d)"),
                             x_rows[bass.ds(n, 1)].rearrange("a p n -> (a p) n")).then_inc(x_in, 16)

            def load_mask(n):
                sp.dma_start(mask_raw[:], mask_rows[bass.ds(n, 1)].broadcast_to([P, S])).then_inc(mask_in, 16)

            def store(n):
                sp.wait_ge(out_ready, n * C + C)
                sp.dma_start(out_rows[bass.ds(n, 1)].rearrange("a p n -> (a p) n"),
                             x_all[:, bass.ds(n, 1)].rearrange("p a t d -> p (a t d)")).then_inc(stored, 16)

            load_x(0)
            row = 0
            for _, vector, rows in vectors:
                sp.dma_start(vec_rows[row:row + rows, :], vector.rearrange("(c p) -> c p", p=P)).then_inc(rows_in, 16)
                row += rows
            sp.dma_start(wk_raw[:], Wk.rearrange("(c p) n -> p c n", p=P)).then_inc(wk_in, 16)
            sp.dma_start(wqv_raw[:, :, 0:D], Wq.rearrange("(c p) n -> p c n", p=P)).then_inc(wqv_in, 16)
            sp.dma_start(wqv_raw[:, :, D:2 * D], Wv.rearrange("(c p) n -> p c n", p=P)).then_inc(wqv_in, 16)
            sp.dma_start(bqv_in[:, 0:D], bq.rearrange("(a d) -> a d", a=1)).then_inc(bias_rows_in, 16)
            sp.dma_start(bqv_in[:, D:2 * D], bv.rearrange("(a d) -> a d", a=1)).then_inc(bias_rows_in, 16)
            load_mask(0)
            sp.dma_start(mask_col[:], mask.rearrange("b (p t) o -> p b (t o)", t=T)).then_inc(maskcol_in, 16)
            sp.dma_start(bo_all[:], b_out.rearrange("(a d) -> a d", a=1).broadcast_to([P, D])).then_inc(bo_in, 16)
            sp.wait_ge(x_in, 16)
            load_x(1)
            sp.dma_start(w_emb[:], W_emb.rearrange("(k p) n -> p k n", p=P)).then_inc(emb_in, 16)
            sp.dma_start(wo_raw[:], W_out.rearrange("(c p) n -> p c n", p=P)).then_inc(wo_in, 16)
            with sp.Fori(2, B) as n:
                sp.wait_ge(x_in, n * 16)
                load_x(n)
            for n in (1, 2):
                sp.wait_ge(mask_ready, n)
                load_mask(n)
            with sp.Fori(3, B) as n:
                sp.wait_ge(mask_ready, n)
                load_mask(n)
                store(n - 3)
            for n in range(B - 3, B - 1):
                store(n)
            for b in range(2):
                sp.wait_ge(out_ready, C * (B - 1) + b + 1)
                tiles = slice(b * T // 2, (b + 1) * T // 2)
                sp.dma_start(out_rows[B - 1][:, tiles.start * D:tiles.stop * D],
                             x_all[:, B - 1, tiles].rearrange("p t d -> p (t d)")).then_inc(stored, 16)
            sp.wait_ge(stored, 16 * (B + 1))

        @program.tensor
        def _(pe):
            def split_product(out_ap, stationary, moving, last=None):
                for c in range(C):
                    s_hi, s_lo = stationary(c)
                    m_hi, m_lo = moving(c)
                    nc.tensor.matmul(out_ap, lhsT=s_hi, rhs=m_hi, start=c == 0, stop=False)
                    nc.tensor.matmul(out_ap, lhsT=s_hi, rhs=m_lo, start=False, stop=False)
                    ins = nc.tensor.matmul(out_ap, lhsT=s_lo, rhs=m_hi, start=False, stop=c == C - 1 and last is None)
                if last is not None:
                    ins = nc.tensor.matmul(out_ap, lhsT=last[0], rhs=last[1], start=False, stop=True)
                return ins

            def tokens(t):
                return slice(t * P, (t + 1) * P)

            def channels(c):
                return slice(c * P, (c + 1) * P)

            def transpose_x(n):
                pe.wait_ge(xhat_ready, n * T + T)
                for c in range(C):
                    for t in range(T):
                        ins = nc.tensor.transpose(bank[XT_BANKS[c]][:, tokens(t)], xhat[:, t, channels(c)], ident[:])
                    ins.then_inc(xT_mm, 1)

            def project_k(n, first=False):
                pe.wait_ge(xT_lo_ready, n * C + C)
                for m in range(C):
                    if m == 1 and not first:
                        pe.wait_ge(y_ready, n * T - T + 1)
                    split_product(bank[K_BANKS[m]][:, :],
                                  lambda c: (wk_hi[:, c, channels(m)], wk_lo[:, c, channels(m)]),
                                  lambda c: (xT_hi[:, c, :], xT_lo[:, c, :])).then_inc(k_mm, 1)

            def project_qv(n, t, first):
                if not first and t < 2:
                    pe.wait_ge(y_ready, n * T - T + t + 2)
                split_product(bank[QV_BANKS[t]][:, :],
                              lambda c: (xT_hi[:, c, tokens(t)], xT_lo[:, c, tokens(t)]),
                              lambda c: (wqv_hi[:, c, :], wqv_lo[:, c, :]),
                              last=(ones[:], bqv_parts[:])).then_inc(qv_mm, 1)

            def transpose_k(n, out):
                if out:
                    pe.wait_ge(out_ready, n * C - C)
                pe.wait_ge(k_exp_ready, n * C + C)
                for t in range(T):
                    for c in range(C):
                        ins = nc.tensor.transpose(bank[KT_BANKS[t // 2]][:, (t % 2) * D + c * P:(t % 2) * D + (c + 1) * P],
                                                  k_exp[:, c, tokens(t)], ident[:])
                    if t % 2 == 1:
                        ins.then_inc(kT_mm, 1)

            def transpose_y(n):
                pe.wait_ge(yhat_ready, n * T + T)
                for c in range(C):
                    for t in range(T):
                        ins = nc.tensor.transpose(bank[YT_BANKS[c]][:, tokens(t)], y_sb[:, t, channels(c)], ident[:])
                    ins.then_inc(yT_mm, 1)

            def transpose_q(n):
                pe.wait_ge(q_exp_ready, n * T + T)
                pe.wait_ge(v_ready, n * T + 2)
                for c in range(C):
                    for t in range(T):
                        ins = nc.tensor.transpose(bank[QT_BANKS[c]][:, tokens(t)], q_exp[:, t, channels(c)], ident[:])
                    ins.then_inc(qT_mm, 1)

            def attend_k_v(n):
                pe.wait_ge(k_ready, n * 2 + 2)
                pe.wait_ge(v_ready, n * T + T)
                for c in range(C):
                    for t in range(T):
                        ins = nc.tensor.matmul(bank[ATT_BANK][:, channels(c)], lhsT=k_sb[:, t, channels(c)],
                                               rhs=v_sb[:, t, channels(c)], start=t == 0, stop=t == T - 1)
                ins.then_inc(att_mm, 1)

            def attend_q(n, first):
                pe.wait_ge(qT_ready, n * C + C)
                pe.wait_ge(att_ready, n * C + C)
                for t in range(T):
                    if t == 3 and not first:
                        pe.wait_ge(tanh_ready, n * C - C + 1)
                    if t == 3 and first:
                        pe.wait_ge(emb_step, 1)
                    for c in range(C):
                        ins = nc.tensor.matmul(bank[Y_BANKS[t]][:, c * (P + HC):(c + 1) * (P + HC)],
                                               lhsT=qT[:, c, tokens(t)], rhs=att[:, c, :], start=True, stop=True)
                    ins.then_inc(y_mm, 1)

            def project_out(n, at_end=False):
                pe.wait_ge(h_lo_ready, n * C + C)
                if at_end:
                    pe.wait_ge(out_ready, n * C)
                else:
                    pe.wait_ge(k_masked, n * C + 3 * C)
                for t in range(T):
                    ins = split_product(bank[O_BANKS[t // 2]][:, (t % 2) * D:(t % 2 + 1) * D],
                                        lambda c: (h_hi[:, c, tokens(t)], h_lo[:, c, tokens(t)]),
                                        lambda c: (wo_hi[:, c, :], wo_lo[:, c, :]))
                    if t % 2 == 1:
                        ins.then_inc(o_mm, 1)

            def bias_products():
                pe.wait_ge(wqv_in, 32)
                for m in range(C):
                    for c in range(C):
                        nc.tensor.matmul(bank[BIAS_COL_BANK][:, m:m + 1], lhsT=wk_raw[:, c, channels(m)],
                                         rhs=ln_b_col[:, c:c + 1], start=c == 0, stop=c == C - 1)
                for c in range(C):
                    ins = nc.tensor.matmul(bank[BIAS_ROW_BANK][0:1, :], lhsT=ln_b_col[:, c:c + 1],
                                           rhs=wqv_raw[:, c, :], start=c == 0, stop=c == C - 1)
                ins.then_inc(bias_mm, 1)

            def embed():
                pe.wait_ge(cond_silu_ready, 1)
                for k in range(KE):
                    ins = nc.tensor.transpose(bank[EMB_T_BANK][:, k * B:(k + 1) * B], cond_silu2[:, k * P:(k + 1) * P],
                                              ident[0:B, 0:B])
                ins.then_inc(cond_T_mm, 1)
                pe.wait_ge(cond_T_ready, 1)
                pe.wait_ge(emb_in, 16)
                for m in range(ME):
                    for k in range(KE):
                        ins = nc.tensor.matmul(bank[EMB_BANK][:, m * B:(m + 1) * B], lhsT=w_emb[:, k, m * P:(m + 1) * P],
                                               rhs=cond_T[:, k, :], start=k == 0, stop=k == KE - 1)
                ins.then_inc(emb_mm, 1)

            def step(i, first=False, out=True, last=False):
                project_qv(i, 0, first)
                project_qv(i, 1, first)
                if out:
                    project_out(i - 2)
                project_qv(i, 2, first)
                project_qv(i, 3, first)
                transpose_k(i, out)
                if first:
                    embed()
                else:
                    transpose_y(i - 1)
                transpose_q(i)
                attend_k_v(i)
                if not last:
                    transpose_x(i + 1)
                attend_q(i, first)
                if not last:
                    project_k(i + 1)

            pe.wait_ge(ident_ready, 1)
            pe.wait_ge(rows_in, 16 * len(vectors))
            nc.tensor.transpose(bank[COLS_BANK][:, 0:VR], vec_rows[:], ident[0:VR, 0:VR]).then_inc(cols_mm, 1)
            pe.wait_ge(cols_ready, 1)
            bias_products()
            transpose_x(0)
            pe.wait_ge(w_lo_ready, 1)
            project_k(0, first=True)
            pe.wait_ge(w_lo_ready, 2)
            pe.wait_ge(bias_ready, 2)
            step(0, first=True, out=False)
            step(1, out=False)
            with pe.Fori(2, B - 1) as i:
                step(i)
            step(B - 1, last=True)
            project_out(B - 2, at_end=True)
            transpose_y(B - 1)
            project_out(B - 1, at_end=True)

        @program.vector
        def _(dve):
            def average(n, stats, mv, step_sem):
                await_then(dve, step_sem, n * 4 + 1)
                for t in range(T):
                    ins = nc.vector.bn_aggr(mv[:, t, :], stats[:, t, :])
                ins.then_inc(step_sem, 1)

            def add_eps(n, mv, var, step_sem):
                dve.wait_ge(step_sem, n * 4 + 2)
                nc.vector.tensor_scalar(var[:], mv[:, :, 1], EPS, None, ALU.add).then_inc(step_sem, 1)

            def halve_bits(n, var, bits, step_sem):
                dve.wait_ge(step_sem, n * 4 + 3)
                nc.vector.tensor_scalar(bits[:], var[:].bitcast(I32), 1, None, ALU.logical_shift_right).then_inc(step_sem, 1)

            def guess(n, bits, rstd, step_sem, seed_sem):
                dve.wait_ge(step_sem, n * 4 + 4)
                nc.vector.tensor_scalar(rstd[:].bitcast(I32), bits[:], -1.0, float(RSQRT_MAGIC), ALU.mult,
                                        ALU.add).then_inc(seed_sem, 1)

            def x_statistics(n):
                dve.wait_ge(x_in, n * 16 + 16)
                for t in range(T):
                    ins = nc.vector.bn_stats(stats1[:, t, :], x_all[:, bass.ds(n, 1), t, :].rearrange("p a d -> p (a d)"))
                ins.then_inc(ln1_step, 1)

            def x_stages(n):
                return [lambda: average(n, stats1, mv1, ln1_step), lambda: add_eps(n, mv1, var1, ln1_step),
                        lambda: halve_bits(n, var1, bits1, ln1_step), lambda: guess(n, bits1, rstd1, ln1_step, seed1)]

            def y_stages(n):
                return [lambda: average(n, stats2, mv2, ln2_step), lambda: add_eps(n, mv2, var2, ln2_step),
                        lambda: halve_bits(n, var2, bits2, ln2_step), lambda: guess(n, bits2, rstd2, ln2_step, seed2)]

            def normalise_x(n):
                dve.wait_ge(rstd1_ready, n + 1)
                for t in range(T):
                    nc.vector.tensor_scalar(xhat[:, t, :], x_all[:, bass.ds(n, 1), t, :].rearrange("p a d -> p (a d)"),
                                            mv1[:, t, 0:1], rstd1[:, t:t + 1], ALU.subtract, ALU.mult).then_inc(xhat_ready, 1)

            def rest_of_xT(n):
                for c in range(C):
                    dve.wait_ge(xT_hi_ready, n * C + c + 1)
                    nc.vector.tensor_tensor(xT_lo[:, c, :], bank[XT_BANKS[c]][:, :], xT_hi[:, c, :].bitcast(F32),
                                            ALU.subtract).then_inc(xT_lo_ready, 1)

            def mask_k(n, c):
                dve.wait_ge(mask_ready, n + 1)
                await_then(dve, k_mm, n * C + c + 1)
                nc.vector.tensor_tensor_reduce(k_exp[:, c, :], bank[K_BANKS[c]][:, :],
                                               mask_add[:].rearrange("p t s -> p (t s)"), 1.0, LOWEST,
                                               ALU.add, ALU.max, k_max[:, c:c + 1]).then_inc(k_masked, 1)

            def shift_k(n):
                dve.wait_ge(k_masked, n * C + C)
                nc.vector.tensor_tensor(k_shift[:], k_max[:], bk_col[:], ALU.add).then_inc(k_step, 1)

            def bias_k(n):
                dve.wait_ge(k_step, n + 1)
                nc.vector.tensor_tensor(k_bias[:], bk_col[:], k_shift[:], ALU.subtract).then_inc(k_bias_ready, 1)

            def shift_q(n, t):
                q = bank[QV_BANKS[t]][:, 0:D].rearrange("p (h d) -> p h d", h=HEADS)
                dve.wait_ge(qv_mm, n * T + t + 1)
                nc.vector.tensor_reduce(q_max[:, t, :], q, AX.X, ALU.max).then_inc(q_max_ready, 1)
                dve.wait_ge(q_max_ready, n * T + t + 1)
                nc.vector.tensor_tensor(q_exp[:, t, :].rearrange("p (h d) -> p h d", h=HEADS), q,
                                        q_max[:, t, :].unsqueeze(2).to_broadcast([P, HEADS, DH]),
                                        ALU.subtract).then_inc(q_shifted, 1)

            def normalise_att(n):
                dve.wait_ge(k_exp_ready, n * C + C)
                nc.vector.reciprocal(k_rsum[:], k_sum[:]).then_inc(rsum_ready, 1)
                dve.wait_ge(rsum_ready, n + 1)
                dve.wait_ge(att_mm, n + 1)
                for c in range(C):
                    nc.vector.scalar_tensor_tensor(out=att[:, c, 0:P], in0=bank[ATT_BANK][:, c * P:(c + 1) * P],
                                                   scalar=k_rsum[:, c:c + 1], in1=head_block[:].rearrange("p h d -> p (h d)"),
                                                   op0=ALU.mult, op1=ALU.mult).then_inc(att_ready, 1)

            def normalise_y(n):
                for t in range(T):
                    y = bank[Y_BANKS[t]][:, 0:C * (P + HC)].rearrange("p (c n) -> p c n", c=C)
                    dve.wait_ge(y_mm, n * T + t + 1)
                    nc.vector.reciprocal(q_rsum[:, t, :].rearrange("p (c h) -> p c h", c=C), y[:, :, P:P + HC]).then_inc(y_rsum_ready, 1)
                    dve.wait_ge(y_rsum_ready, n * T + t + 1)
                    nc.vector.tensor_tensor(y_sb[:, t, :].rearrange("p (c h d) -> p c h d", c=C, h=HC),
                                            y[:, :, 0:P].rearrange("p c (h d) -> p c h d", h=HC),
                                            q_rsum[:, t, :].rearrange("p (c h) -> p c h", c=C).unsqueeze(3).to_broadcast([P, C, HC, DH]),
                                            ALU.mult).then_inc(y_ready, 1)

            def y_statistics(n):
                for t in range(T):
                    dve.wait_ge(y_ready, n * T + t + 1)
                    ins = nc.vector.bn_stats(stats2[:, t, :], y_sb[:, t, :])
                ins.then_inc(ln2_step, 1)

            def gate_h(n, c):
                dve.wait_ge(tanh_ready, n * C + c + 1)
                nc.vector.scalar_tensor_tensor(out=h_full[:, c, :], in0=h_tanh[:, c, :], scalar=1.0, in1=h_full[:, c, :],
                                               op0=ALU.add, op1=ALU.mult).then_inc(h_ready, 1)

            def add_out(n, b):
                dve.wait_ge(x_biased, n + 1)
                dve.wait_ge(o_mm, n * 2 + b + 1)
                rows = x_all[:, bass.ds(n, 1), 2 * b:2 * b + 2, :].rearrange("p a t d -> p (a t d)")
                nc.vector.tensor_tensor(rows, bank[O_BANKS[b]][:, :], rows, ALU.add).then_inc(out_ready, 1)

            def rest_of_weights(lo, full, hi, order):
                dve.wait_ge(w_hi_ready, order)
                nc.vector.tensor_tensor(lo[:], full[:], hi[:].bitcast(F32), ALU.subtract).then_inc(w_lo_ready, 1)

            def scale_weights():
                dve.wait_ge(cols_mm, 1)
                nc.vector.tensor_copy(vec_cols[:], bank[COLS_BANK][:, 0:VR]).then_inc(cols_ready, 1)
                dve.wait_ge(cols_ready, 1)
                dve.wait_ge(wk_in, 16)
                for c in range(C):
                    ins = nc.vector.tensor_scalar(wk_s[:, c, :], wk_raw[:, c, :], ln_w_col[:, c:c + 1], None, ALU.mult)
                ins.then_inc(w_scaled, 1)
                dve.wait_ge(wqv_in, 32)
                for c in range(C):
                    ins = nc.vector.tensor_scalar(wqv_s[:, c, :], wqv_raw[:, c, :], ln_w_col[:, c:c + 1], None, ALU.mult)
                ins.then_inc(w_scaled, 1)

            def biases():
                dve.wait_ge(bias_mm, 1)
                dve.wait_ge(bias_rows_in, 32)
                dve.wait_ge(consts_ready, 1)
                nc.vector.tensor_tensor(bk_col[:], bank[BIAS_COL_BANK][:, 0:C], bk_in[:], ALU.add).then_inc(bias_ready, 1)
                nc.vector.tensor_tensor(bqv_row[:], bank[BIAS_ROW_BANK][0:1, :], bqv_in[:], ALU.add).then_inc(bias_step, 1)
                dve.wait_ge(bias_step, 1)
                nc.vector.tensor_copy(bqv_parts[0:1, :], bqv_row[:]).then_inc(bias_step, 1)
                dve.wait_ge(bias_step, 2)
                nc.vector.tensor_tensor(bqv_parts[32:33, :], bqv_row[:], bqv_parts[0:1, :].bitcast(F32),
                                        ALU.subtract).then_inc(bias_ready, 1)

            def silu_cond():
                dve.wait_ge(cond_tanh_ready, 1)
                nc.vector.scalar_tensor_tensor(out=cond_silu2[:], in0=cond_tanh[:], scalar=1.0, in1=cond_sb[:],
                                               op0=ALU.add, op1=ALU.mult).then_inc(cond_silu_ready, 1)

            def copy_cond_T():
                dve.wait_ge(cond_T_mm, 1)
                nc.vector.tensor_copy(cond_T[:].rearrange("p k b -> p (k b)"), bank[EMB_T_BANK][:, 0:KE * B]).then_inc(cond_T_ready, 1)

            def modulation():
                dve.wait_ge(emb_mm, 1)
                for m in range(ME):
                    ins = nc.vector.tensor_scalar(emb_T[:, m, :], bank[EMB_BANK][:, m * B:(m + 1) * B], 0.5, b_emb_col[:, m:m + 1],
                                                  ALU.mult, ALU.add)
                ins.then_inc(emb_step, 1)
                dve.wait_ge(emb_step, 1)
                nc.vector.tensor_scalar(half_gain[:], emb_T[:, 0:C, :], 1.0, 0.5, ALU.add, ALU.mult)
                nc.vector.tensor_scalar(half_shift[:], emb_T[:, C:2 * C, :], 0.5, None, ALU.mult).then_inc(emb_step, 1)
                dve.wait_ge(emb_step, 2)
                for c in range(C):
                    nc.vector.tensor_scalar(mod_scale[:, c, :], half_gain[:, c, :], ln2_w_col[:, c:c + 1], None, ALU.mult)
                    ins = nc.vector.scalar_tensor_tensor(out=mod_shift[:, c, :], in0=half_gain[:, c, :], scalar=ln2_b_col[:, c:c + 1],
                                                         in1=half_shift[:, c, :], op0=ALU.mult, op1=ALU.add)
                ins.then_inc(mod_ready, 1)

            def step(i, first=False, out=True, stats=True, last=False):
                x_stage, y_stage = x_stages(i + 2), y_stages(i)
                shift_q(i, 0)
                shift_q(i, 1)
                if not last:
                    normalise_x(i + 1)
                if out:
                    add_out(i - 2, 0)
                    add_out(i - 2, 1)
                shift_q(i, 2)
                shift_q(i, 3)
                if stats:
                    x_statistics(i + 2)
                    x_stage[0]()
                if first:
                    copy_cond_T()
                    modulation()
                if not first:
                    gate_h(i - 1, 0)
                if stats:
                    x_stage[1]()
                normalise_att(i)
                if stats:
                    x_stage[2]()
                if not last:
                    rest_of_xT(i + 1)
                if stats:
                    x_stage[3]()
                normalise_y(i)
                if not first:
                    gate_h(i - 1, 1)
                y_statistics(i)
                if not last:
                    mask_k(i + 1, 0)
                y_stage[0]()
                if not last:
                    mask_k(i + 1, 1)
                y_stage[1]()
                if not last:
                    shift_k(i + 1)
                y_stage[2]()
                if not last:
                    bias_k(i + 1)
                y_stage[3]()

            x_statistics(0)
            for stage in x_stages(0):
                stage()
            silu_cond()
            scale_weights()
            rest_of_weights(wk_lo, wk_s, wk_hi, 1)
            rest_of_weights(wqv_lo, wqv_s, wqv_hi, 2)
            normalise_x(0)
            biases()
            rest_of_xT(0)
            x_statistics(1)
            for stage in x_stages(1):
                stage()
            for c in range(C):
                mask_k(0, c)
            shift_k(0)
            bias_k(0)
            step(0, first=True, out=False)
            rest_of_weights(wo_lo, wo_raw, wo_hi, 3)
            step(1, out=False)
            with dve.Fori(2, B - 2) as i:
                step(i)
            step(B - 2, stats=False)
            step(B - 1, stats=False, last=True)
            for b in range(2):
                add_out(B - 2, b)
            for c in range(C):
                gate_h(B - 1, c)
            for b in range(2):
                add_out(B - 1, b)

        @program.scalar
        def _(act):
            def split_hi_x(n):
                for c in range(C):
                    act.wait_ge(xT_mm, n * C + c + 1)
                    nc.scalar.activation(xT_hi[:, c, :], bank[XT_BANKS[c]][:, :], ACT.Copy).then_inc(xT_hi_ready, 1)

            def exp_k(n):
                act.wait_ge(k_bias_ready, n + 1)
                for c in range(C):
                    nc.scalar.activation(k_exp[:, c, :], k_exp[:, c, :], ACT.Exp, bias=k_bias[:, c:c + 1],
                                         accum_out=k_sum[:, c:c + 1]).then_inc(k_exp_ready, 1)

            def exp_q_and_mask_v(n, t):
                act.wait_ge(q_shifted, n * T + t + 1)
                nc.scalar.activation(q_exp[:, t, :], q_exp[:, t, :], ACT.Exp).then_inc(q_exp_ready, 1)
                nc.scalar.activation(v_sb[:, t, :], bank[QV_BANKS[t]][:, D:2 * D], ACT.Copy,
                                     scale=mask_col[:, bass.ds(n, 1), t:t + 1].rearrange("p a t -> p (a t)")).then_inc(v_ready, 1)

            def normalise_y(n):
                act.wait_ge(y_bias_ready, n + 1)
                for t in range(T):
                    nc.scalar.activation(y_sb[:, t, :], y_sb[:, t, :], ACT.Identity, scale=rstd2[:, t:t + 1],
                                         bias=y_bias[:, t:t + 1]).then_inc(yhat_ready, 1)

            def copy_k(n):
                for b in range(2):
                    act.wait_ge(kT_mm, n * 2 + b + 1)
                    nc.scalar.activation(k_sb[:, 2 * b:2 * b + 2, :].rearrange("p t d -> p (t d)"), bank[KT_BANKS[b]][:, :],
                                         ACT.Copy).then_inc(k_ready, 1)

            def copy_qT(n):
                for c in range(C):
                    act.wait_ge(qT_mm, n * C + c + 1)
                    nc.scalar.activation(qT[:, c, :], bank[QT_BANKS[c]][:, :], ACT.Copy).then_inc(qT_ready, 1)

            def modulate(n, c):
                scale = mod_scale[:, c, bass.ds(n, 1)]
                shift = mod_shift[:, c, bass.ds(n, 1)]
                act.wait_ge(yT_mm, n * C + c + 1)
                nc.scalar.activation(h_full[:, c, :], bank[YT_BANKS[c]][:, :], ACT.Identity, scale=scale, bias=shift)
                nc.scalar.activation(h_tanh[:, c, :], bank[YT_BANKS[c]][:, :], ACT.Tanh, scale=scale, bias=shift).then_inc(tanh_ready, 1)

            def split_hi_h(n):
                for c in range(C):
                    act.wait_ge(h_ready, n * C + c + 1)
                    nc.scalar.activation(h_hi[:, c, :], h_full[:, c, :], ACT.Copy).then_inc(h_hi_ready, 1)

            def step(i, first=False, last=False):
                exp_q_and_mask_v(i, 0)
                exp_q_and_mask_v(i, 1)
                if not first:
                    normalise_y(i - 1)
                exp_q_and_mask_v(i, 2)
                exp_q_and_mask_v(i, 3)
                copy_k(i)
                if not first:
                    modulate(i - 1, 0)
                copy_qT(i)
                if not last:
                    split_hi_x(i + 1)
                if not first:
                    modulate(i - 1, 1)
                    split_hi_h(i - 1)
                if not last:
                    exp_k(i + 1)

            act.dma_start(cond_sb[:], cond).then_inc(cond_in, 16)
            act.wait_ge(cond_in, 16)
            nc.scalar.activation(cond_tanh[:], cond_sb[:], ACT.Tanh, scale=0.5).then_inc(cond_tanh_ready, 1)
            act.wait_ge(w_scaled, 1)
            nc.scalar.activation(wk_hi[:], wk_s[:], ACT.Copy).then_inc(w_hi_ready, 1)
            act.wait_ge(w_scaled, 2)
            nc.scalar.activation(wqv_hi[:], wqv_s[:], ACT.Copy).then_inc(w_hi_ready, 1)
            split_hi_x(0)
            act.wait_ge(wo_in, 16)
            nc.scalar.activation(wo_hi[:], wo_raw[:], ACT.Copy).then_inc(w_hi_ready, 1)
            act.wait_ge(maskcol_in, 16)
            exp_k(0)
            step(0, first=True)
            act.wait_ge(mod_ready, 1)
            with act.Fori(1, B - 1) as i:
                step(i)
            step(B - 1, last=True)
            normalise_y(B - 1)
            for c in range(C):
                modulate(B - 1, c)
            split_hi_h(B - 1)

        @program.gpsimd
        def _(pool):
            def prepare_mask(n, again=True):
                pool.wait_ge(mask_in, n * 16 + 16)
                if again:
                    await_then(pool, k_masked, n * C)
                nc.gpsimd.tensor_scalar(mask_add[:], mask_raw[:].rearrange("p (s t) -> p t s", t=T), -1.0, -MASKED,
                                        ALU.add, ALU.mult).then_inc(mask_ready, 1)

            def newton(n, var, rstd, work, seed_sem, step_sem, ready_sem):
                steps = NEWTON * NEWTON_OPS - 1
                pool.wait_ge(seed_sem, n + 1)
                for s in range(NEWTON):
                    at = s * NEWTON_OPS
                    if s:
                        pool.wait_ge(step_sem, n * steps + at)
                    nc.gpsimd.tensor_tensor(work[:], rstd[:], rstd[:], ALU.mult).then_inc(step_sem, 1)
                    pool.wait_ge(step_sem, n * steps + at + 1)
                    nc.gpsimd.tensor_tensor(work[:], work[:], var[:], ALU.mult).then_inc(step_sem, 1)
                    await_then(pool, step_sem, n * steps + at + 2)
                    nc.gpsimd.tensor_scalar(work[:], work[:], -0.5, 1.5, ALU.mult, ALU.add).then_inc(step_sem, 1)
                    pool.wait_ge(step_sem, n * steps + at + 3)
                    ins = nc.gpsimd.tensor_tensor(rstd[:], rstd[:], work[:], ALU.mult)
                    ins.then_inc(step_sem if s < NEWTON - 1 else ready_sem, 1)

            def newton_x(n):
                newton(n, var1, rstd1, newt1, seed1, newton1_step, rstd1_ready)

            def newton_y(n):
                newton(n, var2, rstd2, newt2, seed2, newton2_step, rstd2_ready)
                pool.wait_ge(rstd2_ready, n + 1)
                nc.gpsimd.tensor_tensor(mean_rstd[:], mv2[:, :, 0], rstd2[:], ALU.mult).then_inc(mean_rstd_ready, 1)
                await_then(pool, mean_rstd_ready, n + 1)
                nc.gpsimd.tensor_scalar(y_bias[:], mean_rstd[:], -1.0, None, ALU.mult).then_inc(y_bias_ready, 1)

            def bias_x(n):
                pool.wait_ge(xhat_ready, n * T + T)
                rows = x_all[:, bass.ds(n, 1), :, :].rearrange("p a t d -> p (a t) d")
                nc.gpsimd.tensor_tensor(rows, rows, bo_all[:].unsqueeze(1).to_broadcast([P, T, D]), ALU.add).then_inc(x_biased, 1)

            def rest_of_h(n):
                for c in range(C):
                    pool.wait_ge(h_hi_ready, n * C + c + 1)
                    nc.gpsimd.tensor_tensor(h_lo[:, c, :], h_full[:, c, :], h_hi[:, c, :].bitcast(F32),
                                            ALU.subtract).then_inc(h_lo_ready, 1)

            def step(i, first=False, stats=True, last=False):
                if not last:
                    prepare_mask(i + 1)
                    bias_x(i + 1)
                if stats:
                    newton_x(i + 2)
                if not first:
                    rest_of_h(i - 1)
                newton_y(i)

            nc.gpsimd.memset(ident[:], 0.0).then_inc(ident_zero, 1)
            pool.wait_ge(ident_zero, 1)
            nc.gpsimd.affine_select(out=ident[:], in_=ident[:], compare_op=ALU.not_equal, fill=1.0, base=0,
                                    pattern=[[-1, P]], channel_multiplier=1).then_inc(ident_ready, 1)
            nc.gpsimd.memset(ones[:].bitcast(F32), 1.0)
            nc.gpsimd.memset(bqv_parts[:].bitcast(F32), 0.0)
            nc.gpsimd.memset(head_block[:], 0.0)
            nc.gpsimd.memset(att[:], 0.0).then_inc(ident_zero, 1)
            pool.wait_ge(ident_zero, 2)
            for h in range(HC):
                nc.gpsimd.memset(head_block[h * DH:(h + 1) * DH, h, :], 1.0)
                ins = nc.gpsimd.memset(att[h * DH:(h + 1) * DH, :, P + h:P + h + 1], 1.0)
            ins.then_inc(consts_ready, 1)
            pool.wait_ge(consts_ready, 1)
            newton_x(0)
            prepare_mask(0, again=False)
            pool.wait_ge(bo_in, 16)
            bias_x(0)
            newton_x(1)
            step(0, first=True)
            with pool.Fori(1, B - 2) as i:
                step(i)
            step(B - 2, stats=False)
            step(B - 1, stats=False, last=True)
            rest_of_h(B - 1)


_INS = ["x", "cond_2048", "mask_BxSx1_fk1", "L0_cond_ln_w", "L0_cond_ln_b", "L0_cond_Wq", "L0_cond_bq", "L0_cond_Wk",
        "L0_cond_bk", "L0_cond_Wv", "L0_cond_bv", "L0_cond_W_emb", "L0_cond_b_emb", "L0_cond_ln2_w", "L0_cond_ln2_b",
        "L0_cond_W_out", "L0_cond_b_out"]


def kernel(**inputs):
    import numpy as np
    import concourse.bacc as bacc
    from concourse.bass_utils import run_bass_kernel_spmd

    nc = bacc.Bacc("TRN2", target_bir_lowering=False, num_devices=1)
    arrays, args = {}, []
    for name in _INS:
        a = np.ascontiguousarray(inputs[name])
        arrays[f"in_{name}"] = a
        args.append(nc.dram_tensor(f"in_{name}", a.shape, mybir.dt.from_np(a.dtype), kind="ExternalInput").ap())
    shape = np.asarray(inputs["x"]).shape
    out = nc.dram_tensor("out", shape, F32, kind="ExternalOutput").ap()
    block(nc, *args, out)
    r = run_bass_kernel_spmd(nc, [arrays], core_ids=[0])
    return r.results[0]["out"]
```

```python
from contextlib import ExitStack

import concourse.bass as bass
from concourse import mybir

ALU = mybir.AluOpType
ACT = mybir.ActivationFunctionType
AX = mybir.AxisListType
F32 = mybir.dt.float32
F32R = mybir.dt.float32r
I32 = mybir.dt.int32

P = 128
HEADS = 8
EPS = 1e-5
MASKED = -1000000.0
LOWEST = -3.0e38
RSQRT_MAGIC = 0x5F3759DF
NEWTON = 3
NEWTON_OPS = 4


def block(nc, x, cond, mask, ln_w, ln_b, Wq, bq, Wk, bk, Wv, bv, W_emb, b_emb, ln2_w, ln2_b, W_out, b_out, out):
    B, S, D = x.shape
    TE = cond.shape[1]
    T = S // P
    C = D // P
    DH = D // HEADS
    HC = P // DH
    KE = TE // P
    ME = 2 * D // P
    assert T == 4 and C == 2 and DH == 32 and B >= 4

    x_rows = x.rearrange("b (p t) d -> b p (t d)", t=T)
    out_rows = out.rearrange("b (p t) d -> b p (t d)", t=T)
    mask_rows = mask.rearrange("b s o -> b (s o)")

    with ExitStack() as ctx:
        def sb(name, shape, dt=F32):
            return ctx.enter_context(nc.sbuf_tensor(name, shape, dt))

        def sem(name):
            return ctx.enter_context(nc.semaphore(name))

        bank = [ctx.enter_context(nc.psum_tensor(f"bank{n}", [P, 512], F32)) for n in range(8)]
        K_BANKS = [0, 1]
        QV_BANKS = [2, 3, 4, 5]
        KT_BANKS = [0, 1]
        YT_BANKS = [6, 7]
        QT_BANKS = [2, 3]
        ATT_BANK = 0
        XT_BANKS = [4, 5]
        O_BANKS = [0, 1]
        Y_BANKS = [1, 2, 3, 6]
        LAST_O_BANKS = [2, 3, 4, 5]
        COLS_BANK, COND_T_BANK, BIAS_COL_BANK, BIAS_ROW_BANK = 0, 1, 7, 6
        EMB_BANK = 7

        ident = sb("ident", [P, P])
        head_block = sb("head_block", [P, HC, DH])
        ones = sb("ones", [P, P], F32R)
        wk_raw = sb("wk_raw", [P, C, D])
        wk_hi, wk_lo = sb("wk_hi", [P, C, D], F32R), sb("wk_lo", [P, C, D], F32R)
        wqv_raw = sb("wqv_raw", [P, C, 2 * D])
        wqv_hi, wqv_lo = sb("wqv_hi", [P, C, 2 * D], F32R), sb("wqv_lo", [P, C, 2 * D], F32R)
        wo_raw = sb("wo_raw", [P, C, D])
        wo_hi, wo_lo = sb("wo_hi", [P, C, D], F32R), sb("wo_lo", [P, C, D], F32R)
        vectors = [("ln_w", ln_w, C), ("ln_b", ln_b, C), ("bk", bk, C), ("ln2_w", ln2_w, C), ("ln2_b", ln2_b, C),
                   ("b_emb", b_emb, ME)]
        VR = sum(rows for _, _, rows in vectors)
        vec_rows, vec_cols = sb("vec_rows", [VR, P]), sb("vec_cols", [P, VR])
        col, at = {}, 0
        for name, _, rows in vectors:
            col[name] = vec_cols[:, at:at + rows]
            at += rows
        ln_w_col, ln_b_col, bk_in, ln2_w_col, ln2_b_col, b_emb_col = (
            col[name] for name in ("ln_w", "ln_b", "bk", "ln2_w", "ln2_b", "b_emb"))
        bk_col = sb("bk_col", [P, C])
        bqv_in = sb("bqv_in", [1, 2 * D])
        bqv_row = sb("bqv_row", [1, 2 * D])
        bqv_parts = sb("bqv_parts", [P, 2 * D], F32R)
        bo_all = sb("bo_all", [P, D])
        w_emb = sb("w_emb", [P, KE, 2 * D])
        cond_sb, cond_tanh, cond_silu2 = sb("cond_sb", [B, TE]), sb("cond_tanh", [B, TE]), sb("cond_silu2", [B, TE])
        cond_T = sb("cond_T", [P, KE, B])
        emb_T = sb("emb_T", [P, ME, B])
        half_gain, half_shift = sb("half_gain", [P, C, B]), sb("half_shift", [P, C, B])
        mod_scale, mod_shift = sb("mod_scale", [P, C, B]), sb("mod_shift", [P, C, B])
        mask_col = sb("mask_col", [P, B, T])

        x_all = sb("x_all", [P, B, T, D])
        mask_raw, mask_add = sb("mask_raw", [P, S]), sb("mask_add", [P, T, P])
        stats1, mv1, var1, rstd1, newt1 = (sb("stats1", [P, T, 6]), sb("mv1", [P, T, 2]), sb("var1", [P, T]),
                                           sb("rstd1", [P, T]), sb("newt1", [P, T]))
        stats2, mv2, var2, rstd2, newt2 = (sb("stats2", [P, T, 6]), sb("mv2", [P, T, 2]), sb("var2", [P, T]),
                                           sb("rstd2", [P, T]), sb("newt2", [P, T]))
        bits1, bits2 = sb("bits1", [P, T], I32), sb("bits2", [P, T], I32)
        xhat = sb("xhat", [P, T, D])
        xT_hi, xT_lo = sb("xT_hi", [P, C, S], F32R), sb("xT_lo", [P, C, S], F32R)
        k_exp = sb("k_exp", [P, C, S])
        k_max, k_shift, k_bias, k_sum, k_rsum = (sb("k_max", [P, C]), sb("k_shift", [P, C]), sb("k_bias", [P, C]),
                                                 sb("k_sum", [P, C]), sb("k_rsum", [P, C]))
        k_sb, v_sb = sb("k_sb", [P, T, D]), sb("v_sb", [P, T, D])
        q_max = sb("q_max", [P, T, HEADS])
        q_exp = sb("q_exp", [P, T, D])
        qT = sb("qT", [P, C, S])
        att = sb("att", [P, C, P + HC])
        q_rsum = sb("q_rsum", [P, T, HEADS])
        y_sb = sb("y_sb", [P, T, D])
        mean_rstd, y_bias = sb("mean_rstd", [P, T]), sb("y_bias", [P, T])
        h_full, h_tanh = sb("h_full", [P, C, S]), sb("h_tanh", [P, C, S])
        h_hi, h_lo = sb("h_hi", [P, C, S], F32R), sb("h_lo", [P, C, S], F32R)
        last_h_hi, last_h_lo = sb("last_h_hi", [P, C, S], F32R), sb("last_h_lo", [P, C, S], F32R)

        x_in, half_x_in, mask_in, stored = sem("x_in"), sem("half_x_in"), sem("mask_in"), sem("stored")
        cond_in, wk_in, wqv_in, wo_in, rows_in, bias_rows_in, emb_in, maskcol_in, bo_in = (
            sem("cond_in"), sem("wk_in"), sem("wqv_in"), sem("wo_in"), sem("rows_in"), sem("bias_rows_in"), sem("emb_in"),
            sem("maskcol_in"), sem("bo_in"))
        ident_zero, ident_ready, consts_ready = sem("ident_zero"), sem("ident_ready"), sem("consts_ready")
        cols_mm, cols_ready = sem("cols_mm"), sem("cols_ready")
        w_hi_ready, w_lo_ready, newton_step = sem("w_hi_ready"), sem("w_lo_ready"), sem("newton_step")
        bias_col_mm, bias_row_mm, bias_step, bias_ready = (
            sem("bias_col_mm"), sem("bias_row_mm"), sem("bias_step"), sem("bias_ready"))
        cond_tanh_ready, cond_silu_ready, cond_T_mm, cond_T_ready, emb_mm, emb_step, mod_ready = (
            sem("cond_tanh_ready"), sem("cond_silu_ready"), sem("cond_T_mm"), sem("cond_T_ready"), sem("emb_mm"),
            sem("emb_step"), sem("mod_ready"))
        xT_mm, k_mm, qv_mm, kT_mm, qT_mm, att_mm, y_mm, yT_mm, o_mm = (
            sem("xT_mm"), sem("k_mm"), sem("qv_mm"), sem("kT_mm"), sem("qT_mm"), sem("att_mm"), sem("y_mm"),
            sem("yT_mm"), sem("o_mm"))
        ln1_step, seed1, xhat_ready, xT_lo_ready = sem("ln1_step"), sem("seed1"), sem("xhat_ready"), sem("xT_lo_ready")
        k_masked, k_step, k_bias_ready = sem("k_masked"), sem("k_step"), sem("k_bias_ready")
        q_max_ready, q_shifted = sem("q_max_ready"), sem("q_shifted")
        k_low_ready, rsum_ready, att_ready = sem("k_low_ready"), sem("rsum_ready"), sem("att_ready")
        y_rsum_ready, y_ready, ln2_step, seed2 = sem("y_rsum_ready"), sem("y_ready"), sem("ln2_step"), sem("seed2")
        h_ready, out_ready = sem("h_ready"), sem("out_ready")
        z_ready, last_h_lo_ready = sem("z_ready"), sem("last_h_lo_ready")
        xT_hi_ready, k_exp_ready, q_exp_ready, v_ready, k_high_ready, qT_ready, tanh_ready, h_hi_ready = (
            sem("xT_hi_ready"), sem("k_exp_ready"), sem("q_exp_ready"), sem("v_ready"), sem("k_high_ready"),
            sem("qT_ready"), sem("tanh_ready"), sem("h_hi_ready"))
        mask_ready, newton1_step, rstd1_ready, newton2_step, rstd2_ready, yhat_ready, h_lo_ready, x_biased = (
            sem("mask_ready"), sem("newton1_step"), sem("rstd1_ready"), sem("newton2_step"), sem("rstd2_ready"),
            sem("yhat_ready"), sem("h_lo_ready"), sem("x_biased"))
        mean_rstd_ready, y_bias_ready = sem("mean_rstd_ready"), sem("y_bias_ready")

        passed = sem("passed")
        program = ctx.enter_context(nc.Block())

        def await_then(eng, semaphore, value):
            eng.wait_ge(semaphore, value)
            eng.sem_inc(passed, 1)

        @program.sync
        def _(sp):
            def load_x(n):
                sp.dma_start(x_all[:, bass.ds(n, 1)].rearrange("p a t d -> p (a t d)"),
                             x_rows[bass.ds(n, 1)].rearrange("a p n -> (a p) n")).then_inc(x_in, 16)

            def load_mask(n):
                sp.dma_start(mask_raw[:], mask_rows[bass.ds(n, 1)].broadcast_to([P, S])).then_inc(mask_in, 16)

            def store(n):
                sp.wait_ge(out_ready, n * C + C)
                sp.dma_start(out_rows[bass.ds(n, 1)].rearrange("a p n -> (a p) n"),
                             x_all[:, bass.ds(n, 1)].rearrange("p a t d -> p (a t d)")).then_inc(stored, 16)

            half = T // 2
            for b, arrived in enumerate((half_x_in, x_in)):
                sp.dma_start(x_all[:, 0, b * half:(b + 1) * half, :].rearrange("p t d -> p (t d)"),
                             x_rows[0][:, b * half * D:(b + 1) * half * D]).then_inc(arrived, 16)
            row = 0
            for _, vector, rows in vectors:
                sp.dma_start(vec_rows[row:row + rows, :], vector.rearrange("(c p) -> c p", p=P)).then_inc(rows_in, 16)
                row += rows
            sp.dma_start(wk_raw[:], Wk.rearrange("(c p) n -> p c n", p=P)).then_inc(wk_in, 16)
            sp.dma_start(wqv_raw[:, :, 0:D], Wq.rearrange("(c p) n -> p c n", p=P)).then_inc(wqv_in, 16)
            sp.dma_start(wqv_raw[:, :, D:2 * D], Wv.rearrange("(c p) n -> p c n", p=P)).then_inc(wqv_in, 16)
            sp.dma_start(bqv_in[:, 0:D], bq.rearrange("(a d) -> a d", a=1)).then_inc(bias_rows_in, 16)
            sp.dma_start(bqv_in[:, D:2 * D], bv.rearrange("(a d) -> a d", a=1)).then_inc(bias_rows_in, 16)
            load_mask(0)
            sp.dma_start(mask_col[:], mask.rearrange("b (p t) o -> p b (t o)", t=T)).then_inc(maskcol_in, 16)
            sp.dma_start(bo_all[:], b_out.rearrange("(a d) -> a d", a=1).broadcast_to([P, D])).then_inc(bo_in, 16)
            sp.wait_ge(x_in, 16)
            load_x(1)
            sp.dma_start(w_emb[:], W_emb.rearrange("(k p) n -> p k n", p=P)).then_inc(emb_in, 16)
            sp.dma_start(wo_raw[:], W_out.rearrange("(c p) n -> p c n", p=P)).then_inc(wo_in, 16)
            sp.wait_ge(mask_ready, 1)
            load_mask(1)
            with sp.Fori(2, B) as n:
                sp.wait_ge(x_in, n * 16)
                load_x(n)
            sp.wait_ge(mask_ready, 2)
            load_mask(2)
            with sp.Fori(3, B) as n:
                sp.wait_ge(mask_ready, n)
                load_mask(n)
                store(n - 3)
            for n in range(B - 3, B - 1):
                store(n)
            for b in range(2):
                sp.wait_ge(out_ready, C * (B - 1) + b + 1)
                tiles = slice(b * T // 2, (b + 1) * T // 2)
                sp.dma_start(out_rows[B - 1][:, tiles.start * D:tiles.stop * D],
                             x_all[:, B - 1, tiles].rearrange("p t d -> p (t d)")).then_inc(stored, 16)
            sp.wait_ge(stored, 16 * (B + 1))

        @program.tensor
        def _(pe):
            def split_product(out_ap, stationary, moving, last=None, before=None):
                for c in range(C):
                    if before is not None:
                        before(c)
                    s_hi, s_lo = stationary(c)
                    m_hi, m_lo = moving(c)
                    nc.tensor.matmul(out_ap, lhsT=s_hi, rhs=m_hi, start=c == 0, stop=False)
                    nc.tensor.matmul(out_ap, lhsT=s_hi, rhs=m_lo, start=False, stop=False)
                    ins = nc.tensor.matmul(out_ap, lhsT=s_lo, rhs=m_hi, start=False, stop=c == C - 1 and last is None)
                if last is not None:
                    if before is not None:
                        before(C)
                    ins = nc.tensor.matmul(out_ap, lhsT=last[0], rhs=last[1], start=False, stop=True)
                return ins

            def tokens(t):
                return slice(t * P, (t + 1) * P)

            def channels(c):
                return slice(c * P, (c + 1) * P)

            def first_transpose_x():
                for t in range(T):
                    pe.wait_ge(xhat_ready, t + 1)
                    for c in range(C):
                        ins = nc.tensor.transpose(bank[XT_BANKS[c]][:, tokens(t)], xhat[:, t, channels(c)], ident[:])
                        if t == T - 1:
                            ins.then_inc(xT_mm, 1)

            def transpose_x(n):
                pe.wait_ge(xhat_ready, n * T + T)
                for c in range(C):
                    for t in range(T):
                        ins = nc.tensor.transpose(bank[XT_BANKS[c]][:, tokens(t)], xhat[:, t, channels(c)], ident[:])
                    ins.then_inc(xT_mm, 1)

            def project_k(n):
                pe.wait_ge(xT_lo_ready, n * C + C)
                for m in range(C):
                    if m == 1:
                        pe.wait_ge(y_ready, n * T - T + 1)
                    split_product(bank[K_BANKS[m]][:, :],
                                  lambda c: (wk_hi[:, c, channels(m)], wk_lo[:, c, channels(m)]),
                                  lambda c: (xT_hi[:, c, :], xT_lo[:, c, :])).then_inc(k_mm, 1)

            def first_project_k_hi():
                for m in range(C):
                    for c in range(C):
                        if m == 0:
                            pe.wait_ge(xT_hi_ready, c + 1)
                        for w in (wk_hi, wk_lo):
                            nc.tensor.matmul(bank[K_BANKS[m]][:, :], lhsT=w[:, c, channels(m)], rhs=xT_hi[:, c, :],
                                             start=c == 0 and w is wk_hi, stop=False)

            def first_project_k_lo():
                pe.wait_ge(xT_lo_ready, C)
                for m in range(C):
                    for c in range(C):
                        ins = nc.tensor.matmul(bank[K_BANKS[m]][:, :], lhsT=wk_hi[:, c, channels(m)],
                                               rhs=xT_lo[:, c, :], start=False, stop=c == C - 1)
                    ins.then_inc(k_mm, 1)

            def project_qv(n, t, first):
                def await_bias(c):
                    if c == C:
                        pe.wait_ge(bias_ready, 1)

                if not first and t < 2:
                    pe.wait_ge(y_ready, n * T - T + t + 2)
                split_product(bank[QV_BANKS[t]][:, :],
                              lambda c: (xT_hi[:, c, tokens(t)], xT_lo[:, c, tokens(t)]),
                              lambda c: (wqv_hi[:, c, :], wqv_lo[:, c, :]),
                              last=(ones[:], bqv_parts[:]), before=await_bias if first and t == 0 else None).then_inc(qv_mm, 1)

            def transpose_k(n, out):
                if out:
                    pe.wait_ge(out_ready, n * C - C)
                pe.wait_ge(k_exp_ready, n * C + C)
                for t in range(T):
                    for c in range(C):
                        ins = nc.tensor.transpose(bank[KT_BANKS[t // 2]][:, (t % 2) * D + c * P:(t % 2) * D + (c + 1) * P],
                                                  k_exp[:, c, tokens(t)], ident[:])
                    if t % 2 == 1:
                        ins.then_inc(kT_mm, 1)

            def transpose_y(n, first=False):
                if first:
                    pe.wait_ge(emb_step, 1)
                pe.wait_ge(yhat_ready, n * T + T)
                for c in range(C):
                    for t in range(T):
                        ins = nc.tensor.transpose(bank[YT_BANKS[c]][:, tokens(t)], y_sb[:, t, channels(c)], ident[:])
                    ins.then_inc(yT_mm, 1)

            def transpose_q(n):
                pe.wait_ge(q_exp_ready, n * T + T)
                pe.wait_ge(v_ready, n * T + 2)
                for c in range(C):
                    for t in range(T):
                        ins = nc.tensor.transpose(bank[QT_BANKS[c]][:, tokens(t)], q_exp[:, t, channels(c)], ident[:])
                    ins.then_inc(qT_mm, 1)

            def attend_k_v(n):
                pe.wait_ge(k_low_ready, n + 1)
                pe.wait_ge(k_high_ready, n + 1)
                pe.wait_ge(v_ready, n * T + T)
                for c in range(C):
                    for t in range(T):
                        ins = nc.tensor.matmul(bank[ATT_BANK][:, channels(c)], lhsT=k_sb[:, t, channels(c)],
                                               rhs=v_sb[:, t, channels(c)], start=t == 0, stop=t == T - 1)
                ins.then_inc(att_mm, 1)

            def attend_q(n, first):
                pe.wait_ge(qT_ready, n * C + C)
                for t in range(T):
                    if t == 3 and not first:
                        pe.wait_ge(tanh_ready, n * C - C + 1)
                    for c in range(C):
                        if t == 0:
                            pe.wait_ge(att_ready, n * C + c + 1)
                        ins = nc.tensor.matmul(bank[Y_BANKS[t]][:, c * (P + HC):(c + 1) * (P + HC)],
                                               lhsT=qT[:, c, tokens(t)], rhs=att[:, c, :], start=True, stop=True)
                    ins.then_inc(y_mm, 1)

            def project_out_half(b):
                for t in (2 * b, 2 * b + 1):
                    ins = split_product(bank[O_BANKS[b]][:, (t % 2) * D:(t % 2 + 1) * D],
                                        lambda c: (h_hi[:, c, tokens(t)], h_lo[:, c, tokens(t)]),
                                        lambda c: (wo_hi[:, c, :], wo_lo[:, c, :]))
                ins.then_inc(o_mm, 1)

            def project_out(n):
                pe.wait_ge(h_lo_ready, n * C + C)
                pe.wait_ge(k_masked, n * C + 3 * C)
                for b in range(2):
                    project_out_half(b)

            def last_transpose_y(n):
                for t in range(T):
                    pe.wait_ge(yhat_ready, n * T + t + 1)
                    for c in range(C):
                        ins = nc.tensor.transpose(bank[YT_BANKS[c]][:, tokens(t)], y_sb[:, t, channels(c)], ident[:])
                        if t == T - 1:
                            ins.then_inc(yT_mm, 1)

            def last_project_out(n):
                for c in range(C):
                    pe.wait_ge(h_hi_ready, n * C + c + 1)
                    for t in range(T):
                        o = bank[LAST_O_BANKS[t]][:, 0:D]
                        nc.tensor.matmul(o, lhsT=last_h_hi[:, c, tokens(t)], rhs=wo_hi[:, c, :], start=c == 0, stop=False)
                        nc.tensor.matmul(o, lhsT=last_h_hi[:, c, tokens(t)], rhs=wo_lo[:, c, :], start=False, stop=False)
                pe.wait_ge(h_lo_ready, n * C + 1)
                pe.wait_ge(last_h_lo_ready, 1)
                for t in range(T):
                    for c in range(C):
                        ins = nc.tensor.matmul(bank[LAST_O_BANKS[t]][:, 0:D], lhsT=last_h_lo[:, c, tokens(t)],
                                               rhs=wo_hi[:, c, :], start=False, stop=c == C - 1)
                    ins.then_inc(o_mm, 1)

            def bias_columns():
                pe.wait_ge(wk_in, 16)
                for m in range(C):
                    for c in range(C):
                        ins = nc.tensor.matmul(bank[BIAS_COL_BANK][:, m:m + 1], lhsT=wk_raw[:, c, channels(m)],
                                               rhs=ln_b_col[:, c:c + 1], start=c == 0, stop=c == C - 1)
                ins.then_inc(bias_col_mm, 1)

            def bias_row():
                pe.wait_ge(wqv_in, 32)
                for c in range(C):
                    ins = nc.tensor.matmul(bank[BIAS_ROW_BANK][0:1, :], lhsT=ln_b_col[:, c:c + 1],
                                           rhs=wqv_raw[:, c, :], start=c == 0, stop=c == C - 1)
                ins.then_inc(bias_row_mm, 1)

            def transpose_cond():
                pe.wait_ge(cond_silu_ready, 1)
                for k in range(KE):
                    ins = nc.tensor.transpose(bank[COND_T_BANK][:, k * B:(k + 1) * B], cond_silu2[:, k * P:(k + 1) * P],
                                              ident[0:B, 0:B])
                ins.then_inc(cond_T_mm, 1)

            def embed(m):
                pe.wait_ge(emb_in, 16)
                for k in range(KE):
                    ins = nc.tensor.matmul(bank[EMB_BANK][:, m * B:(m + 1) * B], lhsT=w_emb[:, k, m * P:(m + 1) * P],
                                           rhs=cond_T[:, k, :], start=k == 0, stop=k == KE - 1)
                ins.then_inc(emb_mm, 1)

            def step(i, number=2, last=False):
                first, second = number == 0, number == 1
                for t in range(T):
                    if t == 2 and number >= 2:
                        project_out(i - 2)
                    project_qv(i, t, first)
                    if second:
                        embed(t)
                transpose_k(i, number >= 2)
                if not first:
                    transpose_y(i - 1, second)
                transpose_q(i)
                attend_k_v(i)
                if not last:
                    transpose_x(i + 1)
                attend_q(i, first)
                if not last:
                    project_k(i + 1)

            pe.wait_ge(ident_ready, 1)
            pe.wait_ge(rows_in, 16 * len(vectors))
            nc.tensor.transpose(bank[COLS_BANK][:, 0:VR], vec_rows[:], ident[0:VR, 0:VR]).then_inc(cols_mm, 1)
            pe.wait_ge(cols_ready, 1)
            transpose_cond()
            first_transpose_x()
            pe.wait_ge(w_lo_ready, 1)
            pe.wait_ge(cond_T_ready, 1)
            first_project_k_hi()
            bias_row()
            bias_columns()
            first_project_k_lo()
            pe.wait_ge(w_lo_ready, 2)
            step(0, number=0)
            step(1, number=1)
            with pe.Fori(2, B - 1) as i:
                step(i)
            step(B - 1, last=True)
            pe.wait_ge(h_lo_ready, (B - 2) * C + C)
            project_out_half(0)
            last_transpose_y(B - 1)
            project_out_half(1)
            last_project_out(B - 1)

        @program.vector
        def _(dve):
            def average(n, stats, mv, step_sem):
                await_then(dve, step_sem, n * 4 + 1)
                for t in range(T):
                    ins = nc.vector.bn_aggr(mv[:, t, :], stats[:, t, :])
                ins.then_inc(step_sem, 1)

            def add_eps(n, mv, var, step_sem):
                dve.wait_ge(step_sem, n * 4 + 2)
                nc.vector.tensor_scalar(var[:], mv[:, :, 1], EPS, None, ALU.add).then_inc(step_sem, 1)

            def halve_bits(n, var, bits, step_sem):
                dve.wait_ge(step_sem, n * 4 + 3)
                nc.vector.tensor_scalar(bits[:], var[:].bitcast(I32), 1, None, ALU.logical_shift_right).then_inc(step_sem, 1)

            def guess(n, bits, rstd, step_sem, seed_sem):
                dve.wait_ge(step_sem, n * 4 + 4)
                nc.vector.tensor_scalar(rstd[:].bitcast(I32), bits[:], -1.0, float(RSQRT_MAGIC), ALU.mult,
                                        ALU.add).then_inc(seed_sem, 1)

            def newton_stages(count, var, rstd, work, ready):
                def square():
                    nc.vector.tensor_tensor(work[:], rstd[:], rstd[:], ALU.mult).then_inc(newton_step, 1)

                def half_product():
                    nc.vector.scalar_tensor_tensor(out=work[:], in0=work[:], scalar=-0.5, in1=var[:], op0=ALU.mult,
                                                   op1=ALU.mult).then_inc(newton_step, 1)

                def correct():
                    return nc.vector.scalar_tensor_tensor(out=rstd[:], in0=work[:], scalar=1.5, in1=rstd[:], op0=ALU.add,
                                                          op1=ALU.mult)

                def stage(s, at):
                    if at or s:
                        dve.wait_ge(newton_step, count + 3 * s + at)
                    (square, half_product)[at]()

                def corrected(s):
                    dve.wait_ge(newton_step, count + 3 * s + 2)
                    correct().then_inc(newton_step if s < NEWTON - 1 else ready, 1)

                return [stage_of for s in range(NEWTON) for stage_of in
                        (lambda s=s: stage(s, 0), lambda s=s: stage(s, 1), lambda s=s: corrected(s))]

            def x_statistics(n, halves=False):
                if halves:
                    dve.wait_ge(half_x_in, 16)
                else:
                    dve.wait_ge(x_in, n * 16 + 16)
                for t in range(T):
                    if halves and t == T // 2:
                        dve.wait_ge(x_in, 16)
                    ins = nc.vector.bn_stats(stats1[:, t, :], x_all[:, bass.ds(n, 1), t, :].rearrange("p a d -> p (a d)"))
                ins.then_inc(ln1_step, 1)

            def x_stages(n):
                return [lambda: average(n, stats1, mv1, ln1_step), lambda: add_eps(n, mv1, var1, ln1_step),
                        lambda: halve_bits(n, var1, bits1, ln1_step), lambda: guess(n, bits1, rstd1, ln1_step, seed1)]

            def y_stages(n):
                return [lambda: average(n, stats2, mv2, ln2_step), lambda: add_eps(n, mv2, var2, ln2_step),
                        lambda: halve_bits(n, var2, bits2, ln2_step), lambda: guess(n, bits2, rstd2, ln2_step, seed2)]

            def normalise_x(n):
                dve.wait_ge(rstd1_ready, n + 1)
                for t in range(T):
                    nc.vector.tensor_scalar(xhat[:, t, :], x_all[:, bass.ds(n, 1), t, :].rearrange("p a d -> p (a d)"),
                                            mv1[:, t, 0:1], rstd1[:, t:t + 1], ALU.subtract, ALU.mult).then_inc(xhat_ready, 1)

            def rest_of_xT(n):
                for c in range(C):
                    dve.wait_ge(xT_hi_ready, n * C + c + 1)
                    nc.vector.tensor_tensor(xT_lo[:, c, :], bank[XT_BANKS[c]][:, :], xT_hi[:, c, :].bitcast(F32),
                                            ALU.subtract).then_inc(xT_lo_ready, 1)

            def mask_k(n, c):
                dve.wait_ge(mask_ready, n + 1)
                await_then(dve, k_mm, n * C + c + 1)
                nc.vector.tensor_tensor_reduce(k_exp[:, c, :], bank[K_BANKS[c]][:, :],
                                               mask_add[:].rearrange("p t s -> p (t s)"), 1.0, LOWEST,
                                               ALU.add, ALU.max, k_max[:, c:c + 1]).then_inc(k_masked, 1)

            def shift_k(n):
                dve.wait_ge(k_masked, n * C + C)
                nc.vector.tensor_tensor(k_shift[:], k_max[:], bk_col[:], ALU.add).then_inc(k_step, 1)

            def bias_k(n):
                dve.wait_ge(k_step, n + 1)
                nc.vector.tensor_tensor(k_bias[:], bk_col[:], k_shift[:], ALU.subtract).then_inc(k_bias_ready, 1)

            def shift_q(n, t):
                q = bank[QV_BANKS[t]][:, 0:D].rearrange("p (h d) -> p h d", h=HEADS)
                dve.wait_ge(qv_mm, n * T + t + 1)
                nc.vector.tensor_reduce(q_max[:, t, :], q, AX.X, ALU.max).then_inc(q_max_ready, 1)
                dve.wait_ge(q_max_ready, n * T + t + 1)
                nc.vector.tensor_tensor(q_exp[:, t, :].rearrange("p (h d) -> p h d", h=HEADS), q,
                                        q_max[:, t, :].unsqueeze(2).to_broadcast([P, HEADS, DH]),
                                        ALU.subtract).then_inc(q_shifted, 1)

            def copy_k(n):
                dve.wait_ge(kT_mm, n * 2 + 1)
                nc.vector.tensor_copy(k_sb[:, 0:2, :].rearrange("p t d -> p (t d)"), bank[KT_BANKS[0]][:, :]).then_inc(k_low_ready, 1)

            def invert_k_sum(n):
                dve.wait_ge(k_exp_ready, n * C + C)
                nc.vector.reciprocal(k_rsum[:], k_sum[:]).then_inc(rsum_ready, 1)

            def normalise_att(n):
                dve.wait_ge(rsum_ready, n + 1)
                dve.wait_ge(att_mm, n + 1)
                for c in range(C):
                    nc.vector.scalar_tensor_tensor(out=att[:, c, 0:P], in0=bank[ATT_BANK][:, c * P:(c + 1) * P],
                                                   scalar=k_rsum[:, c:c + 1], in1=head_block[:].rearrange("p h d -> p (h d)"),
                                                   op0=ALU.mult, op1=ALU.mult).then_inc(att_ready, 1)

            def y_parts(t):
                return bank[Y_BANKS[t]][:, 0:C * (P + HC)].rearrange("p (c n) -> p c n", c=C)

            def invert_q_sums(n, t):
                dve.wait_ge(y_mm, n * T + t + 1)
                nc.vector.reciprocal(q_rsum[:, t, :].rearrange("p (c h) -> p c h", c=C),
                                     y_parts(t)[:, :, P:P + HC]).then_inc(y_rsum_ready, 1)

            def divide_y(n, t):
                dve.wait_ge(y_rsum_ready, n * T + t + 1)
                nc.vector.tensor_tensor(y_sb[:, t, :].rearrange("p (c h d) -> p c h d", c=C, h=HC),
                                        y_parts(t)[:, :, 0:P].rearrange("p c (h d) -> p c h d", h=HC),
                                        q_rsum[:, t, :].rearrange("p (c h) -> p c h", c=C).unsqueeze(3).to_broadcast([P, C, HC, DH]),
                                        ALU.mult).then_inc(y_ready, 1)

            def y_statistics(n, t):
                dve.wait_ge(y_ready, n * T + t + 1)
                ins = nc.vector.bn_stats(stats2[:, t, :], y_sb[:, t, :])
                if t == T - 1:
                    ins.then_inc(ln2_step, 1)

            def normalise_y(n):
                invert_q_sums(n, 0)
                for t in range(T):
                    if t < T - 1:
                        invert_q_sums(n, t + 1)
                    divide_y(n, t)

            def normalise_y_with_statistics(n):
                invert_q_sums(n, 0)
                for t in range(T):
                    if t < T - 1:
                        invert_q_sums(n, t + 1)
                    divide_y(n, t)
                    if t:
                        y_statistics(n, t - 1)
                y_statistics(n, T - 1)

            def last_yhat(n):
                dve.wait_ge(rstd2_ready, n + 1)
                for t in range(T):
                    nc.vector.tensor_scalar(y_sb[:, t, :], y_sb[:, t, :], mv2[:, t, 0:1], rstd2[:, t:t + 1],
                                            ALU.subtract, ALU.mult).then_inc(yhat_ready, 1)

            def last_z(n, c):
                dve.wait_ge(yT_mm, n * C + c + 1)
                nc.vector.tensor_scalar(h_full[:, c, :], bank[YT_BANKS[c]][:, :], mod_scale[:, c, n:n + 1],
                                        mod_shift[:, c, n:n + 1], ALU.mult, ALU.add).then_inc(z_ready, 1)

            def last_rest_of_h(n, c):
                dve.wait_ge(h_hi_ready, n * C + c + 1)
                nc.vector.tensor_tensor(last_h_lo[:, c, :], h_full[:, c, :], last_h_hi[:, c, :].bitcast(F32),
                                        ALU.subtract).then_inc(last_h_lo_ready, 1)

            def last_add_out(n, t):
                dve.wait_ge(o_mm, n * 2 + t + 1)
                ins = nc.vector.tensor_tensor(x_all[:, n, t, :], bank[LAST_O_BANKS[t]][:, 0:D], x_all[:, n, t, :], ALU.add)
                if t % 2:
                    ins.then_inc(out_ready, 1)

            def copy_qT(n):
                for c in range(C):
                    dve.wait_ge(qT_mm, n * C + c + 1)
                    nc.vector.tensor_copy(qT[:, c, :], bank[QT_BANKS[c]][:, :]).then_inc(qT_ready, 1)

            def gate_h(n, c):
                dve.wait_ge(tanh_ready, n * C + c + 1)
                nc.vector.scalar_tensor_tensor(out=h_full[:, c, :], in0=h_tanh[:, c, :], scalar=1.0, in1=h_full[:, c, :],
                                               op0=ALU.add, op1=ALU.mult).then_inc(h_ready, 1)

            def add_out(n, b):
                dve.wait_ge(x_biased, n + 1)
                dve.wait_ge(o_mm, n * 2 + b + 1)
                rows = x_all[:, bass.ds(n, 1), 2 * b:2 * b + 2, :].rearrange("p a t d -> p (a t d)")
                nc.vector.tensor_tensor(rows, bank[O_BANKS[b]][:, :], rows, ALU.add).then_inc(out_ready, 1)

            def rest_of_scaled(lo, raw, hi, order):
                dve.wait_ge(w_hi_ready, order)
                for c in range(C):
                    ins = nc.vector.scalar_tensor_tensor(out=lo[:, c, :], in0=raw[:, c, :], scalar=ln_w_col[:, c:c + 1],
                                                         in1=hi[:, c, :].bitcast(F32), op0=ALU.mult, op1=ALU.subtract)
                ins.then_inc(w_lo_ready, 1)

            def rest_of_wo():
                dve.wait_ge(w_hi_ready, 3)
                nc.vector.tensor_tensor(wo_lo[:], wo_raw[:], wo_hi[:].bitcast(F32), ALU.subtract).then_inc(w_lo_ready, 1)

            def copy_cols():
                dve.wait_ge(cols_mm, 1)
                nc.vector.tensor_copy(vec_cols[:], bank[COLS_BANK][:, 0:VR]).then_inc(cols_ready, 1)

            def key_bias():
                dve.wait_ge(bias_col_mm, 1)
                nc.vector.tensor_tensor(bk_col[:], bank[BIAS_COL_BANK][:, 0:C], bk_in[:], ALU.add).then_inc(bias_ready, 1)

            def query_value_bias():
                dve.wait_ge(bias_row_mm, 1)
                dve.wait_ge(bias_rows_in, 32)
                dve.wait_ge(consts_ready, 1)
                nc.vector.tensor_tensor(bqv_row[:], bank[BIAS_ROW_BANK][0:1, :], bqv_in[:], ALU.add).then_inc(bias_step, 1)
                dve.wait_ge(bias_step, 1)
                nc.vector.tensor_copy(bqv_parts[0:1, :], bqv_row[:]).then_inc(bias_step, 1)
                dve.wait_ge(bias_step, 2)
                nc.vector.tensor_tensor(bqv_parts[32:33, :], bqv_row[:], bqv_parts[0:1, :].bitcast(F32),
                                        ALU.subtract).then_inc(bias_ready, 1)

            def silu_cond():
                dve.wait_ge(cond_tanh_ready, 1)
                nc.vector.scalar_tensor_tensor(out=cond_silu2[:], in0=cond_tanh[:], scalar=1.0, in1=cond_sb[:],
                                               op0=ALU.add, op1=ALU.mult).then_inc(cond_silu_ready, 1)

            def copy_cond_T():
                dve.wait_ge(cond_T_mm, 1)
                nc.vector.tensor_copy(cond_T[:].rearrange("p k b -> p (k b)"), bank[COND_T_BANK][:, 0:KE * B]).then_inc(cond_T_ready, 1)

            def modulation():
                dve.wait_ge(emb_mm, ME)
                for m in range(ME):
                    ins = nc.vector.tensor_scalar(emb_T[:, m, :], bank[EMB_BANK][:, m * B:(m + 1) * B], 0.5, b_emb_col[:, m:m + 1],
                                                  ALU.mult, ALU.add)
                ins.then_inc(emb_step, 1)
                dve.wait_ge(emb_step, 1)
                nc.vector.tensor_scalar(half_gain[:], emb_T[:, 0:C, :], 1.0, 0.5, ALU.add, ALU.mult)
                nc.vector.tensor_scalar(half_shift[:], emb_T[:, C:2 * C, :], 0.5, None, ALU.mult).then_inc(emb_step, 1)
                dve.wait_ge(emb_step, 2)
                for c in range(C):
                    nc.vector.tensor_scalar(mod_scale[:, c, :], half_gain[:, c, :], ln2_w_col[:, c:c + 1], None, ALU.mult)
                    ins = nc.vector.scalar_tensor_tensor(out=mod_shift[:, c, :], in0=half_gain[:, c, :], scalar=ln2_b_col[:, c:c + 1],
                                                         in1=half_shift[:, c, :], op0=ALU.mult, op1=ALU.add)
                ins.then_inc(mod_ready, 1)

            def step(i, number=2, stats=True):
                first, second = number == 0, number == 1
                x_stage, y_stage = x_stages(i + 2), y_stages(i)
                shift_q(i, 0)
                shift_q(i, 1)
                normalise_x(i + 1)
                if number >= 2:
                    add_out(i - 2, 0)
                    add_out(i - 2, 1)
                shift_q(i, 2)
                shift_q(i, 3)
                if second:
                    modulation()
                copy_k(i)
                invert_k_sum(i)
                if stats:
                    x_statistics(i + 2)
                    x_stage[0]()
                if not first:
                    gate_h(i - 1, 0)
                if stats:
                    x_stage[1]()
                normalise_att(i)
                if stats:
                    x_stage[2]()
                rest_of_xT(i + 1)
                if stats:
                    x_stage[3]()
                normalise_y(i)
                if not first:
                    gate_h(i - 1, 1)
                for t in range(T):
                    y_statistics(i, t)
                mask_k(i + 1, 0)
                y_stage[0]()
                mask_k(i + 1, 1)
                y_stage[1]()
                shift_k(i + 1)
                y_stage[2]()
                bias_k(i + 1)
                y_stage[3]()

            def last_step(i):
                shift_q(i, 0)
                shift_q(i, 1)
                add_out(i - 2, 0)
                add_out(i - 2, 1)
                shift_q(i, 2)
                shift_q(i, 3)
                copy_k(i)
                invert_k_sum(i)
                copy_qT(i)
                gate_h(i - 1, 0)
                normalise_att(i)
                gate_h(i - 1, 1)
                normalise_y_with_statistics(i)
                for stage in y_stages(i):
                    stage()
                dve.wait_ge(seed2, i + 1)
                for stage in newton_stages(3 * NEWTON - 1, var2, rstd2, newt2, rstd2_ready):
                    stage()
                last_yhat(i)
                add_out(i - 1, 0)
                last_z(i, 1)
                dve.wait_ge(tanh_ready, i * C + 1)
                last_z(i, 0)
                dve.wait_ge(z_ready, C)
                for c in range(C):
                    gate_h(i, c)
                add_out(i - 1, 1)
                last_rest_of_h(i, 1)
                for t in range(T):
                    last_add_out(i, t)

            x_statistics(0, halves=True)
            for stage in x_stages(0):
                stage()
            silu_cond()
            dve.wait_ge(seed1, 1)
            newton_x = newton_stages(0, var1, rstd1, newt1, rstd1_ready)
            for stage in newton_x[:3]:
                stage()
            copy_cols()
            for stage in newton_x[3:]:
                stage()
            copy_cond_T()
            normalise_x(0)
            rest_of_scaled(wk_lo, wk_raw, wk_hi, 1)
            rest_of_xT(0)
            rest_of_scaled(wqv_lo, wqv_raw, wqv_hi, 2)
            x_statistics(1)
            for stage in x_stages(1):
                stage()
            query_value_bias()
            key_bias()
            for c in range(C):
                mask_k(0, c)
            shift_k(0)
            bias_k(0)
            step(0, number=0)
            rest_of_wo()
            step(1, number=1)
            with dve.Fori(2, B - 2) as i:
                step(i)
            step(B - 2, stats=False)
            last_step(B - 1)

        @program.scalar
        def _(act):
            def split_hi_x(n):
                for c in range(C):
                    act.wait_ge(xT_mm, n * C + c + 1)
                    nc.scalar.activation(xT_hi[:, c, :], bank[XT_BANKS[c]][:, :], ACT.Copy).then_inc(xT_hi_ready, 1)

            def exp_k(n):
                act.wait_ge(k_bias_ready, n + 1)
                for c in range(C):
                    nc.scalar.activation(k_exp[:, c, :], k_exp[:, c, :], ACT.Exp, bias=k_bias[:, c:c + 1],
                                         accum_out=k_sum[:, c:c + 1]).then_inc(k_exp_ready, 1)

            def exp_q_and_mask_v(n, t):
                act.wait_ge(q_shifted, n * T + t + 1)
                nc.scalar.activation(q_exp[:, t, :], q_exp[:, t, :], ACT.Exp).then_inc(q_exp_ready, 1)
                nc.scalar.activation(v_sb[:, t, :], bank[QV_BANKS[t]][:, D:2 * D], ACT.Copy,
                                     scale=mask_col[:, bass.ds(n, 1), t:t + 1].rearrange("p a t -> p (a t)")).then_inc(v_ready, 1)

            def normalise_y(n):
                act.wait_ge(y_bias_ready, n + 1)
                for t in range(T):
                    nc.scalar.activation(y_sb[:, t, :], y_sb[:, t, :], ACT.Identity, scale=rstd2[:, t:t + 1],
                                         bias=y_bias[:, t:t + 1]).then_inc(yhat_ready, 1)

            def copy_k(n):
                act.wait_ge(kT_mm, n * 2 + 2)
                nc.scalar.activation(k_sb[:, 2:4, :].rearrange("p t d -> p (t d)"), bank[KT_BANKS[1]][:, :],
                                     ACT.Copy).then_inc(k_high_ready, 1)

            def copy_qT(n):
                for c in range(C):
                    act.wait_ge(qT_mm, n * C + c + 1)
                    nc.scalar.activation(qT[:, c, :], bank[QT_BANKS[c]][:, :], ACT.Copy).then_inc(qT_ready, 1)

            def modulate(n, c):
                scale = mod_scale[:, c, bass.ds(n, 1)]
                shift = mod_shift[:, c, bass.ds(n, 1)]
                act.wait_ge(yT_mm, n * C + c + 1)
                nc.scalar.activation(h_full[:, c, :], bank[YT_BANKS[c]][:, :], ACT.Identity, scale=scale, bias=shift)
                nc.scalar.activation(h_tanh[:, c, :], bank[YT_BANKS[c]][:, :], ACT.Tanh, scale=scale, bias=shift).then_inc(tanh_ready, 1)

            def split_hi_h(n, h_hi=h_hi):
                for c in range(C):
                    act.wait_ge(h_ready, n * C + c + 1)
                    nc.scalar.activation(h_hi[:, c, :], h_full[:, c, :], ACT.Copy).then_inc(h_hi_ready, 1)

            def step(i, first=False, second=False):
                exp_q_and_mask_v(i, 0)
                exp_q_and_mask_v(i, 1)
                if not first:
                    normalise_y(i - 1)
                exp_q_and_mask_v(i, 2)
                exp_q_and_mask_v(i, 3)
                copy_k(i)
                if second:
                    act.wait_ge(mod_ready, 1)
                if not first:
                    modulate(i - 1, 0)
                copy_qT(i)
                split_hi_x(i + 1)
                if not first:
                    modulate(i - 1, 1)
                    split_hi_h(i - 1)
                exp_k(i + 1)

            def last_step(i):
                exp_q_and_mask_v(i, 0)
                exp_q_and_mask_v(i, 1)
                normalise_y(i - 1)
                exp_q_and_mask_v(i, 2)
                exp_q_and_mask_v(i, 3)
                copy_k(i)
                modulate(i - 1, 0)
                modulate(i - 1, 1)
                split_hi_h(i - 1)
                for c in range(C):
                    act.wait_ge(yT_mm, i * C + c + 1)
                    if c == 1:
                        act.wait_ge(z_ready, 1)
                    nc.scalar.activation(h_tanh[:, c, :], bank[YT_BANKS[c]][:, :], ACT.Tanh, scale=mod_scale[:, c, i:i + 1],
                                         bias=mod_shift[:, c, i:i + 1]).then_inc(tanh_ready, 1)
                split_hi_h(i, last_h_hi)

            act.dma_start(cond_sb[:], cond).then_inc(cond_in, 16)
            act.wait_ge(cond_in, 16)
            nc.scalar.activation(cond_tanh[:], cond_sb[:], ACT.Tanh, scale=0.5).then_inc(cond_tanh_ready, 1)
            act.wait_ge(cols_ready, 1)
            for arrived, raw, hi in ((16, wk_raw, wk_hi), (32, wqv_raw, wqv_hi)):
                act.wait_ge(wk_in if raw is wk_raw else wqv_in, arrived)
                for c in range(C):
                    ins = nc.scalar.activation(hi[:, c, :], raw[:, c, :], ACT.Copy, scale=ln_w_col[:, c:c + 1])
                ins.then_inc(w_hi_ready, 1)
            split_hi_x(0)
            act.wait_ge(wo_in, 16)
            nc.scalar.activation(wo_hi[:], wo_raw[:], ACT.Copy).then_inc(w_hi_ready, 1)
            act.wait_ge(maskcol_in, 16)
            exp_k(0)
            step(0, first=True)
            step(1, second=True)
            with act.Fori(2, B - 1) as i:
                step(i)
            last_step(B - 1)

        @program.gpsimd
        def _(pool):
            def prepare_mask(n, again=True):
                pool.wait_ge(mask_in, n * 16 + 16)
                if again:
                    await_then(pool, k_masked, n * C)
                nc.gpsimd.tensor_scalar(mask_add[:], mask_raw[:].rearrange("p (s t) -> p t s", t=T), -1.0, -MASKED,
                                        ALU.add, ALU.mult).then_inc(mask_ready, 1)

            def newton(n, var, rstd, work, seed_sem, step_sem, ready_sem):
                steps = NEWTON * NEWTON_OPS - 1
                done = n if var is var2 else n - 1
                pool.wait_ge(seed_sem, n + 1)
                for s in range(NEWTON):
                    at = s * NEWTON_OPS
                    if s:
                        pool.wait_ge(step_sem, done * steps + at)
                    nc.gpsimd.tensor_tensor(work[:], rstd[:], rstd[:], ALU.mult).then_inc(step_sem, 1)
                    pool.wait_ge(step_sem, done * steps + at + 1)
                    nc.gpsimd.tensor_tensor(work[:], work[:], var[:], ALU.mult).then_inc(step_sem, 1)
                    await_then(pool, step_sem, done * steps + at + 2)
                    nc.gpsimd.tensor_scalar(work[:], work[:], -0.5, 1.5, ALU.mult, ALU.add).then_inc(step_sem, 1)
                    pool.wait_ge(step_sem, done * steps + at + 3)
                    ins = nc.gpsimd.tensor_tensor(rstd[:], rstd[:], work[:], ALU.mult)
                    ins.then_inc(step_sem if s < NEWTON - 1 else ready_sem, 1)

            def newton_x(n):
                newton(n, var1, rstd1, newt1, seed1, newton1_step, rstd1_ready)

            def newton_y(n):
                newton(n, var2, rstd2, newt2, seed2, newton2_step, rstd2_ready)
                pool.wait_ge(rstd2_ready, n + 1)
                nc.gpsimd.tensor_tensor(mean_rstd[:], mv2[:, :, 0], rstd2[:], ALU.mult).then_inc(mean_rstd_ready, 1)
                await_then(pool, mean_rstd_ready, n + 1)
                nc.gpsimd.tensor_scalar(y_bias[:], mean_rstd[:], -1.0, None, ALU.mult).then_inc(y_bias_ready, 1)

            def bias_x(n):
                pool.wait_ge(xhat_ready, n * T + T)
                rows = x_all[:, bass.ds(n, 1), :, :].rearrange("p a t d -> p (a t) d")
                nc.gpsimd.tensor_tensor(rows, rows, bo_all[:].unsqueeze(1).to_broadcast([P, T, D]), ALU.add).then_inc(x_biased, 1)

            def rest_of_h(n, h_hi=h_hi, h_lo=h_lo, chunks=C):
                for c in range(chunks):
                    pool.wait_ge(h_hi_ready, n * C + c + 1)
                    nc.gpsimd.tensor_tensor(h_lo[:, c, :], h_full[:, c, :], h_hi[:, c, :].bitcast(F32),
                                            ALU.subtract).then_inc(h_lo_ready, 1)

            def step(i, first=False, stats=True):
                prepare_mask(i + 1)
                bias_x(i + 1)
                if stats:
                    newton_x(i + 2)
                if not first:
                    rest_of_h(i - 1)
                newton_y(i)

            nc.gpsimd.memset(ident[:], 0.0).then_inc(ident_zero, 1)
            pool.wait_ge(ident_zero, 1)
            nc.gpsimd.affine_select(out=ident[:], in_=ident[:], compare_op=ALU.not_equal, fill=1.0, base=0,
                                    pattern=[[-1, P]], channel_multiplier=1).then_inc(ident_ready, 1)
            nc.gpsimd.memset(ones[:].bitcast(F32), 1.0)
            nc.gpsimd.memset(bqv_parts[:].bitcast(F32), 0.0)
            nc.gpsimd.memset(head_block[:], 0.0)
            nc.gpsimd.memset(att[:], 0.0).then_inc(ident_zero, 1)
            pool.wait_ge(ident_zero, 2)
            for h in range(HC):
                nc.gpsimd.memset(head_block[h * DH:(h + 1) * DH, h, :], 1.0)
                ins = nc.gpsimd.memset(att[h * DH:(h + 1) * DH, :, P + h:P + h + 1], 1.0)
            ins.then_inc(consts_ready, 1)
            pool.wait_ge(consts_ready, 1)
            prepare_mask(0, again=False)
            pool.wait_ge(bo_in, 16)
            bias_x(0)
            newton_x(1)
            step(0, first=True)
            with pool.Fori(1, B - 2) as i:
                step(i)
            step(B - 2, stats=False)
            rest_of_h(B - 2)
            rest_of_h(B - 1, last_h_hi, last_h_lo, chunks=1)


_INS = ["x", "cond_2048", "mask_BxSx1_fk1", "L0_cond_ln_w", "L0_cond_ln_b", "L0_cond_Wq", "L0_cond_bq", "L0_cond_Wk",
        "L0_cond_bk", "L0_cond_Wv", "L0_cond_bv", "L0_cond_W_emb", "L0_cond_b_emb", "L0_cond_ln2_w", "L0_cond_ln2_b",
        "L0_cond_W_out", "L0_cond_b_out"]


def kernel(**inputs):
    import numpy as np
    import concourse.bacc as bacc
    from concourse.bass_utils import run_bass_kernel_spmd

    nc = bacc.Bacc("TRN2", target_bir_lowering=False, num_devices=1)
    arrays, args = {}, []
    for name in _INS:
        a = np.ascontiguousarray(inputs[name])
        arrays[f"in_{name}"] = a
        args.append(nc.dram_tensor(f"in_{name}", a.shape, mybir.dt.from_np(a.dtype), kind="ExternalInput").ap())
    shape = np.asarray(inputs["x"]).shape
    out = nc.dram_tensor("out", shape, F32, kind="ExternalOutput").ap()
    block(nc, *args, out)
    r = run_bass_kernel_spmd(nc, [arrays], core_ids=[0])
    return r.results[0]["out"]
```
